# Optimizing a Trainium2 kernel written in Bass

```python
import numpy as np
import jax
import jax.numpy as jnp

def _softmax(x, axis=-1):
    return jax.nn.softmax(x, axis=axis)

def _gelu(x):
    return jax.nn.gelu(x, approximate=True)

def _silu(x):
    return jax.nn.silu(x)

def _sigmoid(x):
    return jax.nn.sigmoid(x)

def _layernorm(x, axis=-1, eps=1e-05):
    m = jnp.mean(x, axis=axis, keepdims=True)
    v = jnp.var(x, axis=axis, keepdims=True)
    return (x - m) / jnp.sqrt(v + eps)

def _scatter_add(tgt, idx, src, axis=0):
    return tgt.at[idx].add(src)

def _segment_sum(src, seg, n):
    return jax.ops.segment_sum(src, seg, n)
kernel_name = 'mk_decoder_postln_d1_seqx_r4_d5492c'

def setup_inputs(seed: int=0):
    np.random.seed(seed)
    _w = jnp.asarray

    def _rec_inputs():
        import jax
        import jax.numpy as jnp
        _rk = jax.random.key(seed)
        x = -0.0002928 + 1 * jax.random.normal(jax.random.fold_in(_rk, 1), (64, 128, 512), jnp.float32)
        _lenS = 128 - jax.random.randint(jax.random.fold_in(_rk, 7), (64,), 0, max(1, 128 // 4) + 1, jnp.int32)
        _lenS2 = 128 - jax.random.randint(jax.random.fold_in(_rk, 8), (64,), 0, max(1, 128 // 4) + 1, jnp.int32)
        _ctx_2048P = jax.random.normal(jax.random.fold_in(_rk, 11), (64, 16, 512), jnp.float32)
        _ctx_2048c = jax.random.dirichlet(jax.random.fold_in(_rk, 511), 0.3 * jnp.ones((16,), jnp.float32), (64, 128))
        _ctx_2048t = jnp.einsum('bsk,bkd->bsd', _ctx_2048c, _ctx_2048P)
        _ctx_2048t = _ctx_2048t * jax.lax.rsqrt(jnp.mean(jnp.square(_ctx_2048t)) + 1e-12) * 0.953939
        ctx_2048 = -1.39393e-06 + 0.999914 * (_ctx_2048t + 0.3 * jax.random.normal(jax.random.fold_in(_rk, 611), (64, 128, 512), jnp.float32))
        return (x, ctx_2048)
    x, ctx_2048 = _rec_inputs()

    def _L0_attn_setup():
        import jax, jax.numpy as jnp
        import numpy as np
        N_EMBD = 512
        N_HEADS = 16
        HEAD_DIM = N_EMBD // N_HEADS
        THETA = 10000.0

        def _rope_tables(seq_len, head_dim):
            inv = 1.0 / THETA ** (jnp.arange(0, head_dim, 2, dtype=jnp.float32) / head_dim)
            pos = jnp.arange(seq_len, dtype=jnp.float32)
            freqs = jnp.outer(pos, inv)
            return (jnp.cos(freqs)[None, :, None, :], jnp.sin(freqs)[None, :, None, :])

        def _apply_rope(t, cos, sin):
            B, S, H, D = t.shape
            tr = t.reshape(B, S, H, D // 2, 2)
            x0, x1 = (tr[..., 0], tr[..., 1])
            r0 = x0 * cos - x1 * sin
            r1 = x0 * sin + x1 * cos
            return jnp.stack([r0, r1], axis=-1).reshape(B, S, H, D)
        key = jax.random.key(seed)
        ks = jax.random.split(key, 9)
        B, S, E = (4, 512, N_EMBD)
        scale = 1.0 / np.sqrt(E)
        inp = {'x': jax.random.normal(ks[0], (B, S, E), dtype=jnp.float32), 'Wq': jax.random.normal(ks[1], (E, E), dtype=jnp.float32) * scale, 'bq': jnp.zeros((E,), dtype=jnp.float32), 'Wk': jax.random.normal(ks[2], (E, E), dtype=jnp.float32) * scale, 'bk': jnp.zeros((E,), dtype=jnp.float32), 'Wv': jax.random.normal(ks[3], (E, E), dtype=jnp.float32) * scale, 'bv': jnp.zeros((E,), dtype=jnp.float32), 'Wo': jax.random.normal(ks[4], (E, E), dtype=jnp.float32) * scale, 'bo': jnp.zeros((E,), dtype=jnp.float32)}
        return inp
    _L0_attn_all = _L0_attn_setup()
    _L0_attn_in = {k: v for k, v in _L0_attn_all.items() if k in ('Wq', 'bq', 'Wk', 'bk', 'Wv', 'bv', 'Wo', 'bo')}
    del _L0_attn_all

    def _L0_xattn_setup():
        import jax, jax.numpy as jnp
        import numpy as np
        B, S, E, NH = (2, 256, 512, 16)
        DH = E // NH
        EPS = 1e-06

        def _mlstm_forward(q, k, v, Wi, bi, Wf, bf, ln_scale):
            b, s, e = q.shape
            nh = Wi.shape[1]
            dh = e // nh
            x = jnp.concatenate([q, k, v], axis=-1)
            ig = (x @ Wi + bi).transpose(0, 2, 1)[..., None]
            fg = (x @ Wf + bf).transpose(0, 2, 1)[..., None]
            split = lambda t: t.reshape(b, s, nh, dh).transpose(0, 2, 1, 3)
            qh, kh, vh = (split(q), split(k), split(v))
            log_f = jax.nn.log_sigmoid(fg)
            log_f_cum = jnp.concatenate([jnp.zeros((b, nh, 1, 1), q.dtype), jnp.cumsum(log_f, axis=2)], axis=2)
            fg_mat = log_f_cum - jnp.transpose(log_f_cum, (0, 1, 3, 2))
            ltr = jnp.tril(jnp.ones((s, s), dtype=bool))
            log_fg = jnp.where(ltr, fg_mat[:, :, 1:, 1:], -jnp.inf)
            log_D = log_fg + jnp.transpose(ig, (0, 1, 3, 2))
            max_log_D = jnp.max(log_D, axis=-1, keepdims=True)
            D = jnp.exp(log_D - max_log_D)
            qk = jnp.einsum('bhsd,bhtd->bhst', qh, kh) / jnp.sqrt(jnp.asarray(dh, q.dtype))
            C = qk * D
            normalizer = jnp.maximum(jnp.abs(C.sum(-1, keepdims=True)), jnp.exp(-max_log_D))
            Cn = C / (normalizer + EPS)
            h = jnp.einsum('bhst,bhtd->bhsd', Cn, vh)
            mu = h.mean(-1, keepdims=True)
            var = ((h - mu) ** 2).mean(-1, keepdims=True)
            hn = (h - mu) * jax.lax.rsqrt(var + EPS)
            hn = hn * ln_scale.reshape(1, nh, 1, dh)
            return hn.transpose(0, 2, 1, 3).reshape(b, s, e)
        key = jax.random.key(seed)
        ks = jax.random.split(key, 6)
        q = jax.random.normal(ks[0], (B, S, E), dtype=jnp.float32)
        k = jax.random.normal(ks[1], (B, S, E), dtype=jnp.float32)
        v = jax.random.normal(ks[2], (B, S, E), dtype=jnp.float32)
        Wi = jax.random.normal(ks[3], (3 * E, NH), dtype=jnp.float32) * 0.02
        bi = jax.random.normal(ks[4], (NH,), dtype=jnp.float32) * 0.1
        Wf = jax.random.normal(ks[5], (3 * E, NH), dtype=jnp.float32) * 0.02
        bf = jnp.linspace(3.0, 6.0, NH, dtype=jnp.float32)
        ln_scale = jnp.ones((E,), dtype=jnp.float32)
        return {'q': q, 'k': k, 'v': v, 'Wi': Wi, 'bi': bi, 'Wf': Wf, 'bf': bf, 'ln_scale': ln_scale}
    _L0_xattn_all = _L0_xattn_setup()
    _L0_xattn_in = {k: v for k, v in _L0_xattn_all.items() if k in ('Wi', 'bi', 'Wf', 'bf', 'ln_scale')}
    del _L0_xattn_all

    def _L0_ffn_setup():
        import jax, jax.numpy as jnp
        import numpy as np
        B, T, D = (4, 256, 512)
        N, S, H = (8, 8, 8)
        ETA = 1.0
        key = jax.random.key(seed)
        ks = jax.random.split(key, 9)
        return {'x': jax.random.normal(ks[0], (B, T, D), jnp.float32), 'select_weight': jax.random.normal(ks[1], (N, D, S), jnp.float32) / D, 'select_mean_diff': jax.random.normal(ks[2], (N, D), jnp.float32) / D, 'imp_center': jax.random.normal(ks[3], (N,), jnp.float32), 'imp_slope': jax.random.normal(ks[4], (N,), jnp.float32) * 5.0, 'lora_update': jax.random.normal(ks[5], (N, D, H), jnp.float32) * 0.02, 'lora_degen': jax.random.normal(ks[6], (N, D, H), jnp.float32) * 0.02, 'bias_w': jax.random.normal(ks[7], (N, D), jnp.float32) * 0.02, 'debias_w': jax.random.normal(ks[8], (N, D), jnp.float32) * 0.02}
    _L0_ffn_all = _L0_ffn_setup()
    _L0_ffn_in = {k: v for k, v in _L0_ffn_all.items() if k in ('select_weight', 'select_mean_diff', 'imp_center', 'imp_slope', 'lora_update', 'lora_degen', 'bias_w', 'debias_w')}
    del _L0_ffn_all
    return {'x': x, 'ctx_2048': ctx_2048, 'L0_attn_Wq': _L0_attn_in['Wq'], 'L0_attn_bq': _L0_attn_in['bq'], 'L0_attn_Wk': _L0_attn_in['Wk'], 'L0_attn_bk': _L0_attn_in['bk'], 'L0_attn_Wv': _L0_attn_in['Wv'], 'L0_attn_bv': _L0_attn_in['bv'], 'L0_attn_Wo': _L0_attn_in['Wo'], 'L0_attn_bo': _L0_attn_in['bo'], 'L0_xattn_Wi': _L0_xattn_in['Wi'], 'L0_xattn_bi': _L0_xattn_in['bi'], 'L0_xattn_Wf': _L0_xattn_in['Wf'], 'L0_xattn_bf': _L0_xattn_in['bf'], 'L0_xattn_ln_scale': _L0_xattn_in['ln_scale'], 'L0_ffn_select_weight': _L0_ffn_in['select_weight'], 'L0_ffn_select_mean_diff': _L0_ffn_in['select_mean_diff'], 'L0_ffn_imp_center': _L0_ffn_in['imp_center'], 'L0_ffn_imp_slope': _L0_ffn_in['imp_slope'], 'L0_ffn_lora_update': _L0_ffn_in['lora_update'], 'L0_ffn_lora_degen': _L0_ffn_in['lora_degen'], 'L0_ffn_bias_w': _L0_ffn_in['bias_w'], 'L0_ffn_debias_w': _L0_ffn_in['debias_w']}

def reference(x, ctx_2048, L0_attn_Wq, L0_attn_bq, L0_attn_Wk, L0_attn_bk, L0_attn_Wv, L0_attn_bv, L0_attn_Wo, L0_attn_bo, L0_xattn_Wi, L0_xattn_bi, L0_xattn_Wf, L0_xattn_bf, L0_xattn_ln_scale, L0_ffn_select_weight, L0_ffn_select_mean_diff, L0_ffn_imp_center, L0_ffn_imp_slope, L0_ffn_lora_update, L0_ffn_lora_degen, L0_ffn_bias_w, L0_ffn_debias_w):
    import jax
    import jax.numpy as jnp

    def _L0_attn_ref(x, Wq, bq, Wk, bk, Wv, bv, Wo, bo):
        import jax, jax.numpy as jnp
        import numpy as np
        N_EMBD = 512
        N_HEADS = 16
        HEAD_DIM = N_EMBD // N_HEADS
        THETA = 10000.0

        def _rope_tables(seq_len, head_dim):
            inv = 1.0 / THETA ** (jnp.arange(0, head_dim, 2, dtype=jnp.float32) / head_dim)
            pos = jnp.arange(seq_len, dtype=jnp.float32)
            freqs = jnp.outer(pos, inv)
            return (jnp.cos(freqs)[None, :, None, :], jnp.sin(freqs)[None, :, None, :])

        def _apply_rope(t, cos, sin):
            B, S, H, D = t.shape
            tr = t.reshape(B, S, H, D // 2, 2)
            x0, x1 = (tr[..., 0], tr[..., 1])
            r0 = x0 * cos - x1 * sin
            r1 = x0 * sin + x1 * cos
            return jnp.stack([r0, r1], axis=-1).reshape(B, S, H, D)
        B, S, E = x.shape
        H, D = (N_HEADS, HEAD_DIM)
        q = (x @ Wq.T + bq).reshape(B, S, H, D)
        k = (x @ Wk.T + bk).reshape(B, S, H, D)
        v = (x @ Wv.T + bv).reshape(B, S, H, D)
        cos, sin = _rope_tables(S, D)
        q = _apply_rope(q, cos, sin)
        k = _apply_rope(k, cos, sin)
        qk = jnp.einsum('bshd,bstd->bsht', q, k) / jnp.sqrt(jnp.float32(D))
        att = jax.nn.softmax(qk, axis=-1)
        out = jnp.einsum('bsht,bstd->bshd', att, v)
        out = jnp.swapaxes(out, 1, 2).reshape(B, S, E)
        return out @ Wo.T + bo

    def _L0_xattn_ref(q, k, v, Wi, bi, Wf, bf, ln_scale):
        import jax, jax.numpy as jnp
        import numpy as np
        B, S, E, NH = (2, 256, 512, 16)
        DH = E // NH
        EPS = 1e-06

        def _mlstm_forward(q, k, v, Wi, bi, Wf, bf, ln_scale):
            b, s, e = q.shape
            nh = Wi.shape[1]
            dh = e // nh
            x = jnp.concatenate([q, k, v], axis=-1)
            ig = (x @ Wi + bi).transpose(0, 2, 1)[..., None]
            fg = (x @ Wf + bf).transpose(0, 2, 1)[..., None]
            split = lambda t: t.reshape(b, s, nh, dh).transpose(0, 2, 1, 3)
            qh, kh, vh = (split(q), split(k), split(v))
            log_f = jax.nn.log_sigmoid(fg)
            log_f_cum = jnp.concatenate([jnp.zeros((b, nh, 1, 1), q.dtype), jnp.cumsum(log_f, axis=2)], axis=2)
            fg_mat = log_f_cum - jnp.transpose(log_f_cum, (0, 1, 3, 2))
            ltr = jnp.tril(jnp.ones((s, s), dtype=bool))
            log_fg = jnp.where(ltr, fg_mat[:, :, 1:, 1:], -jnp.inf)
            log_D = log_fg + jnp.transpose(ig, (0, 1, 3, 2))
            max_log_D = jnp.max(log_D, axis=-1, keepdims=True)
            D = jnp.exp(log_D - max_log_D)
            qk = jnp.einsum('bhsd,bhtd->bhst', qh, kh) / jnp.sqrt(jnp.asarray(dh, q.dtype))
            C = qk * D
            normalizer = jnp.maximum(jnp.abs(C.sum(-1, keepdims=True)), jnp.exp(-max_log_D))
            Cn = C / (normalizer + EPS)
            h = jnp.einsum('bhst,bhtd->bhsd', Cn, vh)
            mu = h.mean(-1, keepdims=True)
            var = ((h - mu) ** 2).mean(-1, keepdims=True)
            hn = (h - mu) * jax.lax.rsqrt(var + EPS)
            hn = hn * ln_scale.reshape(1, nh, 1, dh)
            return hn.transpose(0, 2, 1, 3).reshape(b, s, e)
        return _mlstm_forward(q, k, v, Wi, bi, Wf, bf, ln_scale)

    def _L0_ffn_ref(x, select_weight, select_mean_diff, imp_center, imp_slope, lora_update, lora_degen, bias_w, debias_w):
        import jax, jax.numpy as jnp
        import numpy as np
        B, T, D = (4, 256, 512)
        N, S, H = (8, 8, 8)
        ETA = 1.0
        x_diff = x[:, None, :, :] - select_mean_diff[None, :, None, :]
        x_diff = x_diff / jnp.linalg.norm(x_diff, axis=3, keepdims=True)
        cont = jnp.einsum('nds,bntd->bnts', select_weight, x_diff) ** 2
        score = cont.sum(axis=-1)
        gate = jax.nn.sigmoid(imp_slope[None, :, None] * (score - imp_center[None, :, None]))
        sel_scale = gate.max(axis=1)[..., None]
        sel_idx = gate.argmax(axis=1)
        debias = jnp.take(debias_w, sel_idx, axis=0)
        bias = jnp.take(bias_w, sel_idx, axis=0)
        upd = jnp.take(lora_update, sel_idx, axis=0)
        dgn = jnp.take(lora_degen, sel_idx, axis=0)
        x_debias = x - debias
        mod_x = jnp.einsum('btdh,btd->bth', upd, x_debias)
        degen_up = jnp.einsum('btdh,bth->btd', dgn, mod_x)
        mod_x_bias = ETA * (bias + degen_up)
        return (1.0 - sel_scale) * x + sel_scale * mod_x_bias
    x = _layernorm(x + _L0_attn_ref(x, L0_attn_Wq, L0_attn_bq, L0_attn_Wk, L0_attn_bk, L0_attn_Wv, L0_attn_bv, L0_attn_Wo, L0_attn_bo), axis=-1)
    x = _layernorm(x + _L0_xattn_ref(x, ctx_2048, ctx_2048, L0_xattn_Wi, L0_xattn_bi, L0_xattn_Wf, L0_xattn_bf, L0_xattn_ln_scale), axis=-1)
    x = _layernorm(x + _L0_ffn_ref(x, L0_ffn_select_weight, L0_ffn_select_mean_diff, L0_ffn_imp_center, L0_ffn_imp_slope, L0_ffn_lora_update, L0_ffn_lora_degen, L0_ffn_bias_w, L0_ffn_debias_w), axis=-1)
    return x

_drawn_inputs = setup_inputs


def setup_inputs(seed=0):
    import zlib

    import numpy as np

    out = dict(_drawn_inputs(seed))
    spreads = {'L0_attn_bq': (0.0, 0.1),
     'L0_attn_bk': (0.0, 0.1),
     'L0_attn_bv': (0.0, 0.1),
     'L0_attn_bo': (0.0, 0.1),
     'L0_xattn_ln_scale': (1.0, 0.2)}
    factors = {'L0_xattn_bi': 64.0, 'L0_ffn_bias_w': 2.801, 'L0_ffn_debias_w': 64.0}
    for name, (base, spread) in spreads.items():
        noise = np.random.default_rng([zlib.crc32(name.encode()), seed]).standard_normal(out[name].shape)
        drawn = base * np.exp(spread * noise) if base else spread * noise
        out[name] = jnp.asarray(drawn.astype(out[name].dtype))
    for name, factor in factors.items():
        out[name] = (out[name] * factor).astype(out[name].dtype)
    return out
```

```python
from collections import namedtuple
from contextlib import ExitStack

import concourse.bass as bass
from concourse import mybir

ALU = mybir.AluOpType
ACT = mybir.ActivationFunctionType
AX_X = mybir.AxisListType.X
F32 = mybir.dt.float32
BF16 = mybir.dt.bfloat16

P = 128
NT = 64
E = 512
CH = E // P
H = 16
D = E // H
HD = D + 1
G = 16
NX = 8
NR = 8
NW = 2 * NX * NR + NX
NL = NX * NR + NX
LN_EPS = 1e-5
ML_EPS = 1e-6

LAGS = 4
PADS = 4
PEEL = 6


class Tile:

    def __init__(self, k, regs=None, dma=None, u=None):
        self.k, self.regs, self.dma, self.u = k, regs, dma, u

    def older(self, n):
        return Tile(self.k - n, self.regs, self.dma, self.u)

    def parity(self):
        return self.k % 2

    def real(self):
        return self.regs is not None or 0 <= self.k < NT

    def index(self):
        return self.k if self.u is None else self.u * 2 + self.k


def upto(tile, back=0):
    if tile.regs is None:
        return min(max(tile.k + 1 - back, 0), NT)
    return tile.regs[tile.k + 1 - back]


def landed(tile, pieces):
    if tile.dma is None:
        return 16 * pieces * (tile.k // 2 + 1)
    return tile.dma[(pieces, tile.k // 2 + 1)]


def stored(tile):
    return 16 * tile.k if tile.dma is None else tile.dma[("out", tile.k)]


def bass_decoder(nc, x, ctx, wq, wk, wv, wo, bqkv, bo, rope, ident, mask_l, mask_r, head_rows,
                 w_gate, b_gate, ln_scale, w_expert, debias, degen, expert_rows, out):
    with ExitStack() as stack:
        def sb(name, shape, dt=F32):
            return stack.enter_context(nc.sbuf_tensor(name, shape, dt))

        def sem(name):
            return stack.enter_context(nc.semaphore(name))

        w_sb = [sb(f"w{n}_sb", [P, CH, E]) for n in "qkvo"]
        bias_in = sb("bias_in", [1, 3 * E])
        bias3 = sb("bias3", [P, 3 * E], BF16)
        bias_rest = sb("bias_rest", [1, 3 * E])
        bias_mid = sb("bias_mid", [1, 3 * E], BF16)
        ones_bf = sb("ones_bf", [P, P], BF16)
        ones_f = sb("ones_f", [P, P])
        bo_sb = sb("bo_sb", [P, E])
        rope_sb = sb("rope_sb", [P, 4, D])
        id_sb = sb("id_sb", [P, P])
        mask_l_sb = sb("mask_l_sb", [P, P], BF16)
        mask_r_sb = sb("mask_r_sb", [P, 4 * P], BF16)
        head_sb = sb("head_sb", [80, H, P], BF16)
        wg_sb = sb("wg_sb", [P, 3, CH, 2 * H])
        wg_ctx = sb("wg_ctx", [P, CH, 2 * H])
        bg_sb = sb("bg_sb", [P, 2 * H])
        lns_sb = sb("lns_sb", [P, E])
        wx_sb = sb("wx_sb", [P, CH, NW])
        debias_sb = sb("debias_sb", [P, CH, NX])
        wx_prod = sb("wx_prod", [P, CH, NW])
        wx_shift = sb("wx_shift", [P, NW])
        degen_sb = sb("degen_sb", [NL, E])
        xrow_sb = sb("xrow_sb", [P, 3, NX])
        eps_ln = sb("eps_ln", [P, 1])
        half_neg = sb("half_neg", [P, H])
        zeros = sb("zeros", [H, P])

        xb = [sb(f"xb{i}", [P, E]) for i in range(2)]
        xr = [sb(f"xr{i}", [P, E]) for i in range(2)]
        xres = [sb(f"xres{i}", [P, E]) for i in range(2)]
        xT = sb("xT", [P, CH, P])
        rot = [[sb(f"rot{n}{i}", [P, E]) for i in range(2)] for n in "qk"]
        rsum = [sb(f"rsum{n}", [P, E]) for n in "qk"]
        QT = [sb(f"QT{i}", [P, CH, P]) for i in range(2)]
        KT = [sb(f"KT{i}", [P, CH, P]) for i in range(2)]
        VT = sb("VT", [P, CH, P])
        VG = [sb(f"VG{i}", [P, G, HD]) for i in range(2)]
        neg_max = sb("neg_max", [P, G])
        ex = sb("ex", [P, G, P])
        PT = sb("PT", [P, G, P])
        o_rec = sb("o_rec", [P, G])
        On = sb("On", [P, E])
        OT = sb("OT", [P, CH, P])
        r1 = sb("r1", [P, E])
        st1 = sb("st1", [P, 6])
        mv1 = sb("mv1", [P, 2])
        ve1 = sb("ve1", [P, 1])
        rs1 = sb("rs1", [P, 1])
        x1 = [sb(f"x1_{i}", [P, E]) for i in range(2)]
        cb = [sb(f"cb{i}", [P, E]) for i in range(2)]
        c1 = [sb(f"c1_{i}", [P, H, HD]) for i in range(2)]
        x1T = sb("x1T", [P, CH, P])
        cT = sb("cT", [P, CH, P])
        gs = sb("gs", [P, 2 * H])
        g_abs = sb("g_abs", [P, H])
        g_exp = sb("g_exp", [P, H])
        g_ln = sb("g_ln", [P, H])
        log_f = sb("log_f", [P, H])
        Fs = sb("Fs", [H, P])
        a_row = sb("a_row", [H, P])
        M_row = sb("M_row", [H, P])
        FM = sb("FM", [H, P])
        m_rest = sb("m_rest", [H, P])
        m_mid = sb("m_mid", [H, P], BF16)
        Mp = sb("Mp", [80, P], BF16)
        a_col = sb("a_col", [P, H])
        eFM = sb("eFM", [P, H])
        Dx = sb("Dx", [P, 4, CH, P])
        Cs = sb("Cs", [P, 4, CH, P])
        h_n0 = sb("h_n0", [P, H])
        h_n1 = sb("h_n1", [P, H])
        h_n2 = sb("h_n2", [P, H])
        h_rec = sb("h_rec", [P, H])
        hn = sb("hn", [P, H, D])
        h_sum = sb("h_sum", [P, H])
        cen = sb("cen", [P, H, D])
        cen2 = sb("cen2", [P, H, D])
        h_var = sb("h_var", [P, H])
        h_ve = sb("h_ve", [P, H])
        h_rs = sb("h_rs", [P, H])
        y1 = sb("y1", [P, H, D])
        y2 = sb("y2", [P, E])
        r2 = sb("r2", [P, E])
        st2 = sb("st2", [P, 6])
        mv2 = sb("mv2", [P, 2])
        ve2 = sb("ve2", [P, 1])
        rs2 = sb("rs2", [P, 1])
        x2 = [sb(f"x2_{i}", [P, E]) for i in range(2)]
        rs2sq = sb("rs2sq", [P, 1])
        x2sq = [sb(f"x2sq{i}", [P, 1]) for i in range(2)]
        x2T = sb("x2T", [P, CH, P])
        fz = sb("fz", [P, 2 * NX * NR])
        fz2 = sb("fz2", [P, NX, NR])
        f_sc = sb("f_sc", [P, NX])
        f_n1 = sb("f_n1", [P, NX])
        f_n2 = sb("f_n2", [P, NX])
        f_n3 = sb("f_n3", [P, NX])
        f_s = sb("f_s", [P, NX])
        f_u = sb("f_u", [P, NX])
        f_v = sb("f_v", [P, NX])
        f_e = sb("f_e", [P, NX])
        f_e1 = sb("f_e1", [P, NX])
        gate = sb("gate", [P, NX])
        g_max = sb("g_max", [P, 1])
        g_key = sb("g_key", [P, NX])
        g_kmax = sb("g_kmax", [P, 1])
        g_rest = sb("g_rest", [P, 1])
        L = sb("L", [P, NL])
        LT = sb("LT", [NL, P])
        y3 = sb("y3", [P, E])
        st3 = sb("st3", [P, 6])
        mv3 = sb("mv3", [P, 2])
        ve3 = sb("ve3", [P, 1])
        rs3 = sb("rs3", [P, 1])
        yo = sb("yo", [P, E])

        bank = [stack.enter_context(nc.psum_tensor(f"bank{i}", [P, 512], F32)) for i in range(8)]

        once = """const_in ones_set bias_step bias_parts bias_set prod_set shift_ps
            shift_set pads_set""".split()
        each = """xT_ps xT_sb q_ps k_ps v_ps q_rot k_rot q_sum k_sum QT_sb KT_sb VT_sb VG_ps VG_sb xres_sb
            O_rec On_sb OT_ps OT_sb proj_ps r1_sb st1_sb mv1_sb ve1_sb rs1_sb x1_sb
            x1T_ps x1T_sb cT_ps cT_sb c1_sb gate_ps gs_sb gabs_sb gexp_sb gln_sb logf_sb gT_ps
            Fs_sb a_sb M_sb FM_sb Mhi_sb Mrest_sb Mmid2_sb Mp_sb aT_ps acol_sb eFM_sb
            hn0_sb hn1_sb hn2_sb hrec_sb hn_sb hsum_sb cen_sb cen2_sb hvar_sb hve_sb hrs_sb y1_sb y2_sb r2_sb
            st2_sb mv2_sb ve2_sb rs2_sb x2_sb rs2sq_sb
            x2T_ps x2T_sb F_ps fz_sb fz2_sb fn1_sb fn2_sb fn3_sb fs_sb fu_sb fv_sb fe_sb fe1_sb
            gate_sb gmax_sb gkey_sb gkmax_sb oh_sb L_sb LT_ps LT_sb Y_ps y3_sb st3_sb mv3_sb
            ve3_sb rs3_sb yo_sb""".split()
        four = "S_ps max_sb ex_sb PT_ps PT_sb D_ps Dx_sb Dm_sb QK_ps C_sb".split()
        two = "O_ps H_ps x_in c_in r_in".split()
        semaphores = {n: sem(n) for n in once + each + ["y_out"]}
        semaphores |= {n: [sem(f"{n}{j}") for j in range(4)] for n in four}
        semaphores |= {n: [sem(f"{n}{j}") for j in range(2)] for n in two}
        s = namedtuple("Semaphores", semaphores)(**semaphores)

        consts = [
            *[(w_sb[n][:], w.rearrange("(c p) n -> p c n", p=P)) for n, w in enumerate((wq, wk, wv, wo))],
            (bias_in[:], bqkv), (bo_sb[:], bo.broadcast_to([P, E])), (rope_sb[:], rope), (id_sb[:], ident),
            (mask_l_sb[:], mask_l), (mask_r_sb[:], mask_r), (head_sb[:], head_rows),
            (wg_sb[:], w_gate.rearrange("(m c p) n -> p m c n", p=P, c=CH)), (bg_sb[:], b_gate.broadcast_to([P, 2 * H])),
            (lns_sb[:], ln_scale.broadcast_to([P, E])), (wx_sb[:], w_expert.rearrange("(c p) n -> p c n", p=P)),
            (debias_sb[:], debias.rearrange("(c p) n -> p c n", p=P)), (degen_sb[:], degen),
            (xrow_sb[:], expert_rows.unsqueeze(0).broadcast_to([P, 3, NX])),
        ]
        CONST_IN = 16 * len(consts)

        def steps(eng, step):
            for t in range(PEEL):
                step(Tile(t))
            with eng.Fori(PEEL // 2, NT // 2) as u:
                regs = {k: eng.snap(u * 2 + k) for k in range(-LAGS - 1, 3)}
                regs |= {("twice", k): eng.snap(u * 4 + 2 * k) for k in range(0, 2)}
                dma = {(n, k): eng.snap(u * (16 * n) + 16 * n * k) for n in (1, 4) for k in range(-1, 2)}
                dma |= {("out", k): eng.snap(u * 32 + 16 * k) for k in range(-LAGS, -LAGS + 2)}
                for k in range(2):
                    step(Tile(k, regs, dma, u))
            for t in range(NT, NT + LAGS):
                step(Tile(t))

        x_v = x.rearrange("b (s q) e -> b q s e", q=4)
        block = stack.enter_context(nc.Block())

        @block.sync
        def _(sp):
            for dst, src in consts:
                sp.dma_start(dst, src).then_inc(s.const_in, 16)

            def load_x(t):
                for q in range(4):
                    sp.dma_start(xb[t.parity()][32 * q:32 * q + 32, :], x_v[t.index(), q]).then_inc(
                        s.x_in[t.parity()], 16)

            def load_res(t):
                sp.dma_start(xr[t.parity()][:], x[t.index()]).then_inc(s.r_in[t.parity()], 16)

            def load_ctx(t):
                sp.dma_start(cb[t.parity()][:], ctx[t.index()]).then_inc(s.c_in[t.parity()], 16)

            def store(t):
                sp.wait_ge(s.yo_sb, upto(t))
                sp.dma_start(out[t.index()], yo[:]).then_inc(s.y_out, 16)

            load_x(Tile(0))
            load_res(Tile(0))

            def step(a):
                nxt, c, f = a.older(-1), a.older(1), a.older(4)
                if nxt.real() and not (nxt.regs is None and nxt.k >= NT):
                    sp.wait_ge(s.xT_ps, upto(nxt, 2))
                    load_x(nxt)
                    sp.wait_ge(s.xres_sb, upto(nxt, 2))
                    load_res(nxt)
                if c.real():
                    sp.wait_ge(s.cT_ps, upto(c, 2))
                    sp.wait_ge(s.c1_sb, upto(c, 2))
                    load_ctx(c)
                if f.real():
                    store(f)

            for t in range(PEEL):
                step(Tile(t))
            with sp.Fori(PEEL // 2, NT // 2 - 1) as u:
                regs = {k: sp.snap(u * 2 + k) for k in range(-LAGS - 1, 3)}
                for k in range(2):
                    step(Tile(k, regs, None, u))
            for t in range(NT - 2, NT + LAGS):
                step(Tile(t))
            sp.wait_ge(s.y_out, 16 * NT)

        @block.tensor
        def _(pe):
            mm = nc.tensor.matmul

            def transposes(dst, src):
                for c in range(CH):
                    last = nc.tensor.transpose(dst[:, c * P:(c + 1) * P], src[:, c * P:(c + 1) * P], id_sb[:])
                return last

            def p_xT(a):
                pe.wait_ge(s.x_in[a.parity()], landed(a, 4))
                pe.wait_ge(s.C_sb[3], upto(a, 3))
                transposes(bank[4], xb[a.parity()]).then_inc(s.xT_ps, 1)

            def p_proj(a, n, b, out_sem):
                mm(bank[b][:], ones_bf[:], bias3[:, n * E:(n + 1) * E], start=True, stop=False)
                for c in range(CH):
                    last = mm(bank[b][:], xT[:, c, :], w_sb[n][:, c, :], start=False, stop=(c == CH - 1))
                last.then_inc(out_sem, 1)

            def p_q(a):
                pe.wait_ge(s.xT_sb, upto(a))
                pe.wait_ge(s.cT_sb, upto(a, 2))
                p_proj(a, 0, 6, s.q_ps)

            def p_k(a):
                pe.wait_ge(s.hn_sb, upto(a, 3))
                p_proj(a, 1, 4, s.k_ps)

            def p_v(a):
                pe.wait_ge(s.q_rot, upto(a))
                p_proj(a, 2, 6, s.v_ps)

            def p_VG(a):
                pe.wait_ge(s.VT_sb, upto(a))
                pe.wait_ge(s.k_rot, upto(a))
                for c in range(CH):
                    last = nc.tensor.transpose(bank[4][:, c * P:(c + 1) * P],
                                               VT[:, c, :], id_sb[:])
                last.then_inc(s.VG_ps, 1)

            def a_S(b):
                pe.wait_ge(s.QT_sb, upto(b))
                pe.wait_ge(s.KT_sb, upto(b))
                q_v, k_v = QT[b.parity()], KT[b.parity()]
                for j in range(4):
                    pe.wait_ge(s.Dx_sb[j], upto(b, 2))
                    mm(bank[j][:], mask_l_sb[:], mask_r_sb[:], start=True, stop=True, skip_group_check=True)
                    rows = slice(32 * j, 32 * j + 32)
                    for c in range(CH):
                        last = mm(bank[j][:, c * P:(c + 1) * P], q_v[rows, c, :], k_v[rows, c, :],
                                  start=False, stop=True, skip_group_check=True)
                    last.then_inc(s.S_ps[j], 1)

            def a_PT(b):
                for j in range(4):
                    pe.wait_ge(s.ex_sb[j], upto(b))
                    for c in range(CH):
                        last = nc.tensor.transpose(bank[j][:, c * P:(c + 1) * P], ex[:, 4 * j + c, :], id_sb[:])
                    last.then_inc(s.PT_ps[j], 1)

            def a_O(b):
                pe.wait_ge(s.VG_sb, upto(b))
                for m in range(2):
                    pe.wait_ge(*((s.VT_sb, upto(b, -1)) if m == 0 else (s.fn1_sb, upto(b, 3))))
                    for j in (2 * m, 2 * m + 1):
                        pe.wait_ge(s.PT_sb[j], upto(b))
                    for g in range(8 * m, 8 * m + 8):
                        last = mm(bank[6 + m][:, (g % 8) * HD:(g % 8 + 1) * HD], PT[:, g, :],
                                  VG[b.parity()][:, g, :], start=True, stop=True)
                    last.then_inc(s.O_ps[m], 1)

            def a_OT(b):
                pe.wait_ge(s.On_sb, upto(b))
                pe.wait_ge(s.LT_sb, upto(b, 3))
                if b.regs is None:
                    pe.wait_ge(s.acol_sb, upto(b, 1))
                    pe.wait_ge(s.eFM_sb, upto(b, 1))
                transposes(bank[5], On).then_inc(s.OT_ps, 1)

            def a_proj(b):
                pe.wait_ge(s.OT_sb, upto(b))
                for c in range(CH):
                    last = mm(bank[5][:], OT[:, c, :], w_sb[3][:, c, :], start=(c == 0), stop=(c == CH - 1))
                last.then_inc(s.proj_ps, 1)

            def m_T(c):
                pe.wait_ge(s.x1_sb, upto(c))
                pe.wait_ge(s.r1_sb, upto(c))
                transposes(bank[5], x1[c.parity()]).then_inc(s.x1T_ps, 1)
                pe.wait_ge(s.c_in[c.parity()], landed(c, 1))
                pe.wait_ge(s.C_sb[2], upto(c, 1))
                transposes(bank[6], cb[c.parity()]).then_inc(s.cT_ps, 1)

            def m_gate(c):
                pe.wait_ge(s.x1T_sb, upto(c))
                pe.wait_ge(s.cT_sb, upto(c))
                for n in range(CH):
                    mm(bank[5][:, 0:2 * H], x1T[:, n, :], wg_sb[:, 0, n, :],
                       start=(n == 0), stop=False)
                for n in range(CH):
                    last = mm(bank[5][:, 0:2 * H], cT[:, n, :], wg_ctx[:, n, :], start=False, stop=(n == CH - 1))
                last.then_inc(s.gate_ps, 1)

            def m_gT(c):
                pe.wait_ge(s.logf_sb, upto(c))
                nc.tensor.transpose(bank[5][0:H, 0:P], log_f[:], id_sb[:])
                nc.tensor.transpose(bank[5][0:H, P:2 * P], gs[:, 0:H], id_sb[:]).then_inc(s.gT_ps, 1)

            def m_aT(c):
                pe.wait_ge(s.pads_set, PADS)
                pe.wait_ge(s.FM_sb, upto(c))
                nc.tensor.transpose(bank[5][:, 0:H], a_row[:], id_sb[0:H, 0:H])
                nc.tensor.transpose(bank[5][:, H:2 * H], FM[:], id_sb[0:H, 0:H]).then_inc(s.aT_ps, 1)

            def m_D(c):
                pe.wait_ge(s.Mp_sb, upto(c))
                pe.wait_ge(s.Mmid2_sb, upto(c))
                for j in range(4):
                    pe.wait_ge(s.PT_sb[j], upto(c, -1))
                    for n in range(CH):
                        last = mm(bank[j][:, n * P:(n + 1) * P], head_sb[:, 4 * n + j, :], Mp[:],
                                  start=True, stop=True)
                    last.then_inc(s.D_ps[j], 1)

            def m_QK(c, j):
                free = ((s.VG_sb, upto(c, -2)), (s.On_sb, upto(c, -1)), (s.y3_sb, upto(c, 2)), (s.C_sb[0], upto(c)))
                pe.wait_ge(*free[j])
                if j == 1 and c.regs is None:
                    pe.wait_ge(s.fn1_sb, upto(c, 2))
                rows = slice(32 * j, 32 * j + 32)
                b = (4, 7, 6, 4)[j]
                for n in range(CH):
                    last = mm(bank[b][:, n * P:(n + 1) * P], cT[rows, n, :], x1T[rows, n, :], start=True, stop=True)
                last.then_inc(s.QK_ps[j], 1)

            def r_H(e):
                for j in range(4):
                    pe.wait_ge(s.C_sb[j], upto(e))
                pe.wait_ge(s.c1_sb, upto(e))
                for m in range(2):
                    if m == 1:
                        pe.wait_ge(s.xT_sb, upto(e, -3))
                    for h in range(8 * m, 8 * m + 8):
                        last = mm(bank[(7, 4)[m]][:, (h % 8) * HD:(h % 8 + 1) * HD], Cs[:, h % 4, h // 4, :],
                                  c1[e.parity()][:, h, :], start=True, stop=True)
                    last.then_inc(s.H_ps[m], 1)

            def x_x2T(f):
                pe.wait_ge(s.x2_sb, upto(f))
                pe.wait_ge(s.hn_sb, upto(f, -1))
                transposes(bank[7], x2[f.parity()]).then_inc(s.x2T_ps, 1)

            def x_F(f):
                pe.wait_ge(s.x2T_sb, upto(f))
                for c in range(CH):
                    last = mm(bank[7][:, 0:NW], x2T[:, c, :], wx_sb[:, c, :], start=(c == 0), stop=(c == CH - 1))
                last.then_inc(s.F_ps, 1)

            def x_LT(f):
                pe.wait_ge(s.L_sb, upto(f))
                pe.wait_ge(s.oh_sb, upto(f))
                pe.wait_ge(s.acol_sb, upto(f, -2))
                pe.wait_ge(s.eFM_sb, upto(f, -2))
                nc.tensor.transpose(bank[5][0:NL, 0:P], L[:], id_sb[:]).then_inc(s.LT_ps, 1)

            def x_Y(f):
                pe.wait_ge(s.LT_sb, upto(f))
                pe.wait_ge(s.On_sb, upto(f, -3))
                mm(bank[6][:], LT[:], degen_sb[:], start=True, stop=True).then_inc(s.Y_ps, 1)

            def settle(a):
                pe.wait_ge(s.VG_sb, upto(a, 1))
                for j in range(4):
                    pe.wait_ge(s.Dx_sb[j], upto(a, 3))
                    pe.wait_ge(s.C_sb[j], upto(a, 3))
                pe.wait_ge(s.fn1_sb, upto(a, 5))
                pe.wait_ge(s.y3_sb, upto(a, 5))

            pe.wait_ge(s.const_in, CONST_IN)
            pe.wait_ge(s.prod_set, 3)
            pe.wait_ge(s.ones_set, 2)
            for c in range(CH):
                last = mm(bank[0][:, 0:NW], ones_f[:], wx_prod[:, c, :], start=(c == 0), stop=(c == CH - 1))
            last.then_inc(s.shift_ps, 1)
            pe.wait_ge(s.shift_set, 1)
            pe.wait_ge(s.bias_set, 1)
            pe.wait_ge(s.bias_parts, 2)
            pe.wait_ge(s.pads_set, PADS)

            def step(a):
                b, c, e, f = a.older(1), a.older(2), a.older(3), a.older(4)
                if a.regs is None:
                    settle(a)
                if a.real():
                    p_xT(a)
                if b.real():
                    a_S(b)
                if c.real():
                    m_T(c)
                if e.real():
                    r_H(e)
                if c.real():
                    m_gate(c)
                if a.real():
                    p_q(a)
                if f.real():
                    x_x2T(f)
                if a.real():
                    p_k(a)
                if c.real():
                    m_gT(c)
                if a.real():
                    p_v(a)
                if b.real():
                    a_PT(b)
                if f.real():
                    x_F(f)
                if c.real():
                    m_aT(c)
                if a.real():
                    p_VG(a)
                if b.real():
                    a_O(b)
                if f.real():
                    x_LT(f)
                if c.real():
                    m_D(c)
                    m_QK(c, 0)
                if b.real():
                    a_OT(b)
                if f.real():
                    x_Y(f)
                if c.real():
                    m_QK(c, 1)
                    m_QK(c, 2)
                if b.real():
                    a_proj(b)
                if c.real():
                    m_QK(c, 3)

            steps(pe, step)

        @block.scalar
        def _(act):
            def copy4(dst, b):
                return nc.scalar.activation(dst, bank[b][:], ACT.Copy)

            def p_xT(a):
                act.wait_ge(s.xT_ps, upto(a))
                act.wait_ge(s.v_ps, upto(a, 1))
                copy4(xT[:].rearrange("p c n -> p (c n)"), 4).then_inc(s.xT_sb, 1)

            def p_VG(a):
                act.wait_ge(s.VG_ps, upto(a))
                act.wait_ge(s.O_ps[1], upto(a, 2))
                for c in range(CH):
                    last = nc.scalar.activation(
                        VG[a.parity()][:].rearrange("p (q c) d -> p c q d", c=CH)[:, c, :, 0:D],
                        bank[4][:, c * P:(c + 1) * P].rearrange("p (q d) -> p q d", d=D), ACT.Copy)
                last.then_inc(s.VG_sb, 1)

            def a_exp(b, j):
                act.wait_ge(s.max_sb[j], upto(b))
                act.wait_ge(s.PT_ps[j], upto(b, 1))
                for c in range(CH):
                    g = 4 * j + c
                    last = nc.scalar.activation(ex[:, g, :], bank[j][:, c * P:(c + 1) * P], ACT.Exp,
                                                bias=neg_max[:, g:g + 1])
                last.then_inc(s.ex_sb[j], 1)

            def a_PT(b, j):
                act.wait_ge(s.PT_ps[j], upto(b))
                act.wait_ge(s.O_ps[j // 2], upto(b, 1))
                copy4(PT[:, 4 * j:4 * j + 4, :].rearrange("p g m -> p (g m)"), j).then_inc(s.PT_sb[j], 1)

            def a_OT(b):
                act.wait_ge(s.OT_ps, upto(b))
                act.wait_ge(s.proj_ps, upto(b, 1))
                copy4(OT[:].rearrange("p c n -> p (c n)"), 5).then_inc(s.OT_sb, 1)

            def m_T(c):
                act.wait_ge(s.x1T_ps, upto(c))
                act.wait_ge(s.QK_ps[3], upto(c, 1))
                copy4(x1T[:].rearrange("p c n -> p (c n)"), 5).then_inc(s.x1T_sb, 1)
                act.wait_ge(s.cT_ps, upto(c))
                copy4(cT[:].rearrange("p c n -> p (c n)"), 6).then_inc(s.cT_sb, 1)

            def m_gate(c):
                act.wait_ge(s.gabs_sb, upto(c))
                nc.scalar.activation(g_exp[:], g_abs[:], ACT.Exp).then_inc(s.gexp_sb, 1)
                act.wait_ge(s.gexp_sb, upto(c))
                nc.scalar.activation(g_ln[:], g_exp[:], ACT.Ln, bias=1.0).then_inc(s.gln_sb, 1)

            def m_eFM(c):
                act.wait_ge(s.acol_sb, upto(c))
                act.wait_ge(s.hn1_sb, upto(c, 1))
                nc.scalar.activation(eFM[:], bank[5][:, H:2 * H], ACT.Exp, scale=-1.0).then_inc(s.eFM_sb, 1)

            def m_Dx(c, j):
                act.wait_ge(s.D_ps[j], upto(c))
                act.wait_ge(s.acol_sb, upto(c))
                act.wait_ge(s.C_sb[j], upto(c, 1))
                for n in range(CH):
                    h = 4 * n + j
                    last = nc.scalar.activation(Dx[:, j, n, :], bank[j][:, n * P:(n + 1) * P], ACT.Exp,
                                                bias=a_col[:, h:h + 1])
                last.then_inc(s.Dx_sb[j], 1)

            def r_sq(e):
                act.wait_ge(s.cen_sb, upto(e))
                act.wait_ge(s.hvar_sb, upto(e, 1))
                nc.scalar.activation(cen2[:], cen[:], ACT.Square).then_inc(s.cen2_sb, 1)

            def x_x2T(f):
                act.wait_ge(s.x2T_ps, upto(f))
                act.wait_ge(s.F_ps, upto(f, 1))
                copy4(x2T[:].rearrange("p c n -> p (c n)"), 7).then_inc(s.x2T_sb, 1)

            def x_exp(f):
                act.wait_ge(s.fv_sb, upto(f))
                act.wait_ge(s.fe1_sb, upto(f, 1))
                nc.scalar.activation(f_e[:], f_v[:], ACT.Exp, scale=-1.0).then_inc(s.fe_sb, 1)

            act.wait_ge(s.const_in, CONST_IN)

            def step(a):
                b, c, e, f = a.older(1), a.older(2), a.older(3), a.older(4)
                if a.real():
                    p_xT(a)
                if b.real():
                    a_exp(b, 0)
                if c.real():
                    m_T(c)
                if b.real():
                    a_exp(b, 1)
                    a_exp(b, 2)
                    a_exp(b, 3)
                if c.real():
                    m_gate(c)
                if e.real():
                    r_sq(e)
                if f.real():
                    x_x2T(f)
                if b.real():
                    a_PT(b, 2)
                    a_PT(b, 3)
                if f.real():
                    x_exp(f)
                if c.real():
                    m_eFM(c)
                if a.real():
                    p_VG(a)
                if c.real():
                    m_Dx(c, 0)
                    m_Dx(c, 1)
                if b.real():
                    a_OT(b)
                if c.real():
                    m_Dx(c, 2)
                    m_Dx(c, 3)

            steps(act, step)

        @block.gpsimd
        def _(pool):
            tt = nc.gpsimd.tensor_tensor

            def p_xres(a):
                pool.wait_ge(s.r_in[a.parity()], landed(a, 1))
                pool.wait_ge(s.r1_sb, upto(a, 2))
                tt(xres[a.parity()][:], xr[a.parity()][:], bo_sb[:], ALU.add).then_inc(s.xres_sb, 1)

            def p_rot(a, n):
                pool.wait_ge((s.q_rot, s.k_rot)[n], upto(a))
                pool.wait_ge((s.QT_sb, s.KT_sb)[n], upto(a, 1))
                tt(rsum[n][:], rot[n][0][:], rot[n][1][:], ALU.add).then_inc((s.q_sum, s.k_sum)[n], 1)

            def m_c1(c):
                pool.wait_ge(s.c_in[c.parity()], landed(c, 1))
                pool.wait_ge(s.H_ps[1], upto(c, 2))
                tt(c1[c.parity()][:, :, 0:D], cb[c.parity()][:].rearrange("p (h d) -> p h d", d=D),
                   ones_f[:, 0:1].unsqueeze(2).broadcast_to([P, H, D]), ALU.mult).then_inc(s.c1_sb, 1)

            def m_mask(c, j):
                pool.wait_ge(s.pads_set, PADS)
                pool.wait_ge(s.Dx_sb[j], upto(c))
                nc.gpsimd.affine_select(Dx[:, j], Dx[:, j], compare_op=ALU.is_ge, fill=0.0, base=0,
                                        pattern=[[0, CH], [1, P]],
                                        channel_multiplier=-1).then_inc(s.Dm_sb[j], 1)

            def r_head(e):
                pool.wait_ge(s.hve_sb, upto(e))
                pool.wait_ge(s.y1_sb, upto(e, 1))
                tt(h_rs[:], h_ve[:], half_neg[:], ALU.pow).then_inc(s.hrs_sb, 1)
                pool.wait_ge(s.hrs_sb, upto(e))
                pool.wait_ge(s.cen_sb, upto(e))
                pool.wait_ge(s.y2_sb, upto(e, 1))
                tt(y1[:], cen[:], h_rs[:].unsqueeze(2).broadcast_to([P, H, D]), ALU.mult).then_inc(s.y1_sb, 1)
                pool.wait_ge(s.y1_sb, upto(e))
                pool.wait_ge(s.r2_sb, upto(e, 1))
                tt(y2[:], y1[:].rearrange("p h d -> p (h d)"), lns_sb[:], ALU.mult).then_inc(s.y2_sb, 1)
                pool.wait_ge(s.y2_sb, upto(e))
                pool.wait_ge(s.x1_sb, upto(e))
                pool.wait_ge(s.x2_sb, upto(e, 1))
                tt(r2[:], y2[:], x1[e.parity()][:], ALU.add).then_inc(s.r2_sb, 1)

            def rsqrt(t, ve, rs, ve_sem, rs_sem, used):
                pool.wait_ge(ve_sem, upto(t))
                pool.wait_ge(used, upto(t, 1))
                tt(rs[:], ve[:], half_neg[:, 0:1], ALU.pow).then_inc(rs_sem, 1)

            pool.wait_ge(s.const_in, CONST_IN)
            nc.gpsimd.memset(half_neg[:], -0.5).then_inc(s.pads_set, 1)
            for i in range(2):
                nc.gpsimd.memset(VG[i][:], 1.0)
                last = nc.gpsimd.memset(c1[i][:], 1.0)
            last.then_inc(s.pads_set, 1)
            tt(wg_ctx[:], wg_sb[:, 1], wg_sb[:, 2], ALU.add).then_inc(s.pads_set, 1)
            pool.wait_ge(s.pads_set, PADS)
            pool.wait_ge(s.ones_set, 2)

            def step(a):
                b, c, e, f = a.older(1), a.older(2), a.older(3), a.older(4)
                if a.real():
                    p_xres(a)
                if c.real():
                    m_c1(c)
                if a.real():
                    p_rot(a, 0)
                if e.real():
                    r_head(e)
                if a.real():
                    p_rot(a, 1)
                if e.real():
                    rsqrt(e, ve2, rs2, s.ve2_sb, s.rs2_sb, s.x2_sb)
                if c.real():
                    m_mask(c, 0)
                    m_mask(c, 1)
                if f.real():
                    rsqrt(f, ve3, rs3, s.ve3_sb, s.rs3_sb, s.yo_sb)
                if c.real():
                    m_mask(c, 2)
                    m_mask(c, 3)
                if b.real():
                    rsqrt(b, ve1, rs1, s.ve1_sb, s.rs1_sb, s.x1_sb)

            steps(pool, step)

        @block.vector
        def _(dve):
            tt = nc.vector.tensor_tensor
            ts = nc.vector.tensor_scalar
            stt = nc.vector.scalar_tensor_tensor
            red = nc.vector.tensor_reduce

            def rotate(t, n, b, ps, done, summed):
                dve.wait_ge(ps, upto(t))
                dve.wait_ge(summed, upto(t, 1))
                src = bank[b][:].rearrange("p (h d) -> p h d", d=D)
                cos = rope_sb[:, 2 * n, :].unsqueeze(1).broadcast_to([P, H, D])
                sin = rope_sb[:, 2 * n + 1, :].unsqueeze(1).broadcast_to([P, H, D])
                tt(rot[n][0][:].rearrange("p (h d) -> p h d", d=D), src, cos, ALU.mult)
                other = rot[n][1][:].rearrange("p (h d) -> p h d", d=D)
                tt(other[:, :, 0:D // 2], src[:, :, D // 2:D], sin[:, :, 0:D // 2], ALU.mult)
                tt(other[:, :, D // 2:D], src[:, :, 0:D // 2], sin[:, :, D // 2:D], ALU.mult).then_inc(done, 1)

            def p_q(a):
                rotate(a, 0, 6, s.q_ps, s.q_rot, s.q_sum)

            def p_k(a):
                rotate(a, 1, 4, s.k_ps, s.k_rot, s.k_sum)

            def by_group(t):
                return t[:].rearrange("p c (h i) -> p h i c", i=8)

            def p_T(a, n):
                dve.wait_ge((s.q_sum, s.k_sum)[n], upto(a))
                dve.wait_ge(s.S_ps[3], upto(a, 2))
                nc.vector.transpose(by_group((QT, KT)[n][a.parity()]), rsum[n][:]).then_inc((s.QT_sb, s.KT_sb)[n], 1)

            def p_VT(a):
                dve.wait_ge(s.v_ps, upto(a))
                dve.wait_ge(s.VG_ps, upto(a, 1))
                nc.vector.transpose(by_group(VT), bank[6][:]).then_inc(s.VT_sb, 1)

            def a_max(b, j):
                dve.wait_ge(s.S_ps[j], upto(b))
                dve.wait_ge(s.ex_sb[j], upto(b, 1))
                red(neg_max[:, 4 * j:4 * j + 4], bank[j][:].rearrange("p (g n) -> p g n", n=P), AX_X, ALU.max,
                    negate=True).then_inc(s.max_sb[j], 1)

            def a_PT(b, j):
                dve.wait_ge(s.PT_ps[j], upto(b))
                dve.wait_ge(s.O_ps[j // 2], upto(b, 1))
                nc.vector.tensor_copy(PT[:, 4 * j:4 * j + 4, :].rearrange("p g m -> p (g m)"),
                                      bank[j][:]).then_inc(s.PT_sb[j], 1)

            def a_On(b):
                dve.wait_ge(s.OT_ps, upto(b, 1))
                for m in range(2):
                    dve.wait_ge(s.O_ps[m], upto(b))
                    o = bank[6 + m][:, 0:8 * HD].rearrange("p (g d) -> p g d", d=HD)
                    nc.vector.reciprocal(o_rec[:, 8 * m:8 * m + 8], o[:, :, D]).then_inc(s.O_rec, 1)
                dve.wait_ge(s.O_rec, twice(b))
                for m in range(2):
                    o = bank[6 + m][:, 0:8 * HD].rearrange("p (q c d) -> p q c d", d=HD, c=CH)
                    rec = o_rec[:, 8 * m:8 * m + 8].rearrange("p (q c) -> p q c", c=CH)
                    last = tt(On[:].rearrange("p (c q d) -> p q c d", q=4, d=D)[:, 2 * m:2 * m + 2],
                              o[:, :, :, 0:D], rec.unsqueeze(3).broadcast_to([P, 2, CH, D]), ALU.mult)
                last.then_inc(s.On_sb, 1)

            def norm_stats(t, r, st, mv, ve, st_sem, mv_sem, ve_sem):
                nc.vector.bn_stats(st[:], r[:]).then_inc(st_sem, 1)
                dve.wait_ge(s.pads_set, PADS)
                dve.wait_ge(st_sem, upto(t))
                nc.vector.bn_aggr(mv[:], st[:]).then_inc(mv_sem, 1)
                dve.wait_ge(mv_sem, upto(t))
                ts(ve[:], mv[:, 1:2], LN_EPS, None, ALU.add).then_inc(ve_sem, 1)

            def a_r1(b):
                dve.wait_ge(s.proj_ps, upto(b))
                dve.wait_ge(s.xres_sb, upto(b))
                tt(r1[:], bank[5][:], xres[b.parity()][:], ALU.add).then_inc(s.r1_sb, 1)
                dve.wait_ge(s.r1_sb, upto(b))
                norm_stats(b, r1, st1, mv1, ve1, s.st1_sb, s.mv1_sb, s.ve1_sb)

            def a_x1(b):
                dve.wait_ge(s.rs1_sb, upto(b))
                dve.wait_ge(s.r2_sb, upto(b, 2))
                ts(x1[b.parity()][:], r1[:], mv1[:, 0:1], rs1[:], ALU.subtract, ALU.mult).then_inc(s.x1_sb, 1)

            def m_gs(c):
                dve.wait_ge(s.gate_ps, upto(c))
                dve.wait_ge(s.gT_ps, upto(c, 1))
                tt(gs[:], bank[5][:, 0:2 * H], bg_sb[:], ALU.add).then_inc(s.gs_sb, 1)
                dve.wait_ge(s.gs_sb, upto(c))
                stt(out=g_abs[:], in0=gs[:, H:2 * H], scalar=-1.0, in1=gs[:, H:2 * H], op0=ALU.mult,
                    op1=ALU.min).then_inc(s.gabs_sb, 1)

            def m_logf(c):
                dve.wait_ge(s.gln_sb, upto(c))
                stt(out=log_f[:], in0=gs[:, H:2 * H], scalar=0.0, in1=g_ln[:], op0=ALU.min,
                    op1=ALU.subtract).then_inc(s.logf_sb, 1)

            def m_scan(c):
                dve.wait_ge(s.gT_ps, upto(c))
                dve.wait_ge(s.aT_ps, upto(c, 1))
                dve.wait_ge(s.pads_set, PADS)
                nc.vector.tensor_tensor_scan(Fs[:], bank[5][0:H, 0:P], zeros[:], 0.0, ALU.add,
                                             ALU.add).then_inc(s.Fs_sb, 1)
                dve.wait_ge(s.Fs_sb, upto(c))
                tt(a_row[:], bank[5][0:H, P:2 * P], Fs[:], ALU.subtract).then_inc(s.a_sb, 1)
                dve.wait_ge(s.a_sb, upto(c))
                nc.vector.tensor_tensor_scan(M_row[:], a_row[:], a_row[:], -3.0e38, ALU.max,
                                             ALU.max).then_inc(s.M_sb, 1)
                dve.wait_ge(s.M_sb, upto(c))
                tt(FM[:], Fs[:], M_row[:], ALU.add).then_inc(s.FM_sb, 1)
                dve.wait_ge(s.D_ps[3], upto(c, 1))
                ts(Mp[0:H, :], M_row[:], -1.0, None, ALU.mult).then_inc(s.Mhi_sb, 1)
                dve.wait_ge(s.Mhi_sb, upto(c))
                stt(out=m_rest[:], in0=M_row[:], scalar=-1.0, in1=Mp[0:H, :], op0=ALU.mult,
                    op1=ALU.subtract).then_inc(s.Mrest_sb, 1)
                dve.wait_ge(s.Mrest_sb, upto(c))
                nc.vector.tensor_copy(m_mid[:], m_rest[:])
                nc.vector.tensor_copy(Mp[32:32 + H, :], m_rest[:]).then_inc(s.Mmid2_sb, 1)
                dve.wait_ge(s.Mmid2_sb, upto(c))
                tt(Mp[64:64 + H, :], m_rest[:], m_mid[:], ALU.subtract).then_inc(s.Mp_sb, 1)

            def m_acol(c):
                dve.wait_ge(s.aT_ps, upto(c))
                dve.wait_ge(s.Dx_sb[3], upto(c, 1))
                nc.vector.tensor_copy(a_col[:], bank[5][:, 0:H]).then_inc(s.acol_sb, 1)

            def m_C(c, j):
                dve.wait_ge(s.QK_ps[j], upto(c))
                dve.wait_ge(s.Dm_sb[j], upto(c))
                dve.wait_ge(s.H_ps[1], upto(c, 1))
                stt(out=Cs[:, j], in0=bank[(4, 7, 6, 4)[j]][:].rearrange("p (c n) -> p c n", n=P),
                    scalar=float(D) ** -0.5, in1=Dx[:, j], op0=ALU.mult, op1=ALU.mult).then_inc(s.C_sb[j], 1)

            def r_h(e):
                dve.wait_ge(s.eFM_sb, upto(e))
                for m in range(2):
                    dve.wait_ge(s.H_ps[m], upto(e))
                    hs = bank[(7, 4)[m]][:, 0:8 * HD].rearrange("p (h d) -> p h d", d=HD)
                    last = stt(out=h_n0[:, 8 * m:8 * m + 8], in0=hs[:, :, D], scalar=-1.0,
                               in1=eFM[:, 8 * m:8 * m + 8], op0=ALU.mult, op1=ALU.max)
                last.then_inc(s.hn0_sb, 1)
                dve.wait_ge(s.hn0_sb, upto(e))
                for m in range(2):
                    hs = bank[(7, 4)[m]][:, 0:8 * HD].rearrange("p (h d) -> p h d", d=HD)
                    last = tt(h_n1[:, 8 * m:8 * m + 8], hs[:, :, D], h_n0[:, 8 * m:8 * m + 8], ALU.max)
                last.then_inc(s.hn1_sb, 1)
                dve.wait_ge(s.hn1_sb, upto(e))
                ts(h_n2[:], h_n1[:], ML_EPS, None, ALU.add).then_inc(s.hn2_sb, 1)
                dve.wait_ge(s.hn2_sb, upto(e))
                nc.vector.reciprocal(h_rec[:], h_n2[:]).then_inc(s.hrec_sb, 1)
                dve.wait_ge(s.hrec_sb, upto(e))
                for m in range(2):
                    hs = bank[(7, 4)[m]][:, 0:8 * HD].rearrange("p (h d) -> p h d", d=HD)
                    last = tt(hn[:, 8 * m:8 * m + 8, :], hs[:, :, 0:D],
                              h_rec[:, 8 * m:8 * m + 8].unsqueeze(2).broadcast_to([P, 8, D]), ALU.mult)
                last.then_inc(s.hn_sb, 1)
                dve.wait_ge(s.hn_sb, upto(e))
                red(h_sum[:], hn[:], AX_X, ALU.add).then_inc(s.hsum_sb, 1)
                dve.wait_ge(s.hsum_sb, upto(e))
                dve.wait_ge(s.y1_sb, upto(e, 1))
                stt(out=cen[:], in0=h_sum[:].unsqueeze(2).broadcast_to([P, H, D]), scalar=-1.0 / D, in1=hn[:],
                    op0=ALU.mult, op1=ALU.add).then_inc(s.cen_sb, 1)

            def r_var(e):
                dve.wait_ge(s.cen2_sb, upto(e))
                red(h_var[:], cen2[:], AX_X, ALU.add).then_inc(s.hvar_sb, 1)
                dve.wait_ge(s.hvar_sb, upto(e))
                dve.wait_ge(s.hrs_sb, upto(e, 1))
                ts(h_ve[:], h_var[:], 1.0 / D, ML_EPS, ALU.mult, ALU.add).then_inc(s.hve_sb, 1)

            def r_r2(e):
                dve.wait_ge(s.r2_sb, upto(e))
                norm_stats(e, r2, st2, mv2, ve2, s.st2_sb, s.mv2_sb, s.ve2_sb)

            def r_x2(e):
                dve.wait_ge(s.rs2_sb, upto(e))
                tt(rs2sq[:], rs2[:], rs2[:], ALU.mult).then_inc(s.rs2sq_sb, 1)
                dve.wait_ge(s.rs2sq_sb, upto(e))
                ts(x2sq[e.parity()][:], mv2[:, 1:2], rs2sq[:], float(E), ALU.mult, ALU.mult)
                dve.wait_ge(s.x2T_ps, upto(e, 2))
                ts(x2[e.parity()][:], r2[:], mv2[:, 0:1], rs2[:], ALU.subtract, ALU.mult).then_inc(s.x2_sb, 1)

            def x_choose(f):
                dve.wait_ge(s.F_ps, upto(f))
                nw = NX * NR
                tt(fz[:], bank[7][:, 0:2 * nw], wx_shift[:, 0:2 * nw], ALU.subtract).then_inc(s.fz_sb, 1)
                stt(out=f_n1[:], in0=bank[7][:, 2 * nw:NW], scalar=-2.0, in1=wx_shift[:, 2 * nw:NW],
                    op0=ALU.mult, op1=ALU.add).then_inc(s.fn1_sb, 1)
                dve.wait_ge(s.fz_sb, upto(f))
                tt(fz2[:], fz[:, 0:nw].rearrange("p (n r) -> p n r", r=NR),
                   fz[:, 0:nw].rearrange("p (n r) -> p n r", r=NR), ALU.mult).then_inc(s.fz2_sb, 1)
                dve.wait_ge(s.fn1_sb, upto(f))
                dve.wait_ge(s.x2_sb, upto(f))
                ts(f_n2[:], f_n1[:], x2sq[f.parity()][:], None, ALU.add).then_inc(s.fn2_sb, 1)
                dve.wait_ge(s.fz2_sb, upto(f))
                red(f_sc[:], fz2[:], AX_X, ALU.add)
                dve.wait_ge(s.fn2_sb, upto(f))
                nc.vector.reciprocal(f_n3[:], f_n2[:]).then_inc(s.fn3_sb, 1)
                dve.wait_ge(s.fn3_sb, upto(f))
                tt(f_s[:], f_sc[:], f_n3[:], ALU.mult).then_inc(s.fs_sb, 1)
                dve.wait_ge(s.fs_sb, upto(f))
                tt(f_u[:], f_s[:], xrow_sb[:, 0, :], ALU.subtract).then_inc(s.fu_sb, 1)
                dve.wait_ge(s.fu_sb, upto(f))
                tt(f_v[:], f_u[:], xrow_sb[:, 1, :], ALU.mult).then_inc(s.fv_sb, 1)

            def x_gate(f):
                dve.wait_ge(s.fe_sb, upto(f))
                ts(f_e1[:], f_e[:], 1.0, None, ALU.add).then_inc(s.fe1_sb, 1)
                dve.wait_ge(s.fe1_sb, upto(f))
                nc.vector.reciprocal(gate[:], f_e1[:]).then_inc(s.gate_sb, 1)
                dve.wait_ge(s.gate_sb, upto(f))
                red(g_max[:], gate[:], AX_X, ALU.max).then_inc(s.gmax_sb, 1)
                dve.wait_ge(s.gmax_sb, upto(f))
                stt(out=g_key[:], in0=gate[:], scalar=g_max[:], in1=xrow_sb[:, 2, :], op0=ALU.is_equal,
                    op1=ALU.mult).then_inc(s.gkey_sb, 1)
                ts(g_rest[:], g_max[:], -1.0, 2.0, ALU.mult, ALU.add)
                dve.wait_ge(s.gkey_sb, upto(f))
                red(g_kmax[:], g_key[:], AX_X, ALU.max).then_inc(s.gkmax_sb, 1)
                dve.wait_ge(s.gkmax_sb, upto(f))
                dve.wait_ge(s.LT_ps, upto(f, 1))
                ts(L[:, NX * NR:NL], g_key[:], g_kmax[:], g_max[:], ALU.is_equal, ALU.mult).then_inc(s.oh_sb, 1)
                dve.wait_ge(s.oh_sb, upto(f))
                tt(L[:, 0:NX * NR].rearrange("p (n r) -> p n r", r=NR),
                   fz[:, NX * NR:2 * NX * NR].rearrange("p (n r) -> p n r", r=NR),
                   L[:, NX * NR:NL].unsqueeze(2).broadcast_to([P, NX, NR]), ALU.mult).then_inc(s.L_sb, 1)

            def x_LT(f):
                dve.wait_ge(s.LT_ps, upto(f))
                dve.wait_ge(s.Y_ps, upto(f, 1))
                nc.vector.tensor_copy(LT[:], bank[5][0:NL, 0:P]).then_inc(s.LT_sb, 1)

            def x_y3(f):
                dve.wait_ge(s.Y_ps, upto(f))
                dve.wait_ge(s.x2_sb, upto(f))
                stt(out=y3[:], in0=x2[f.parity()][:], scalar=g_rest[:], in1=bank[6][:], op0=ALU.mult,
                    op1=ALU.add).then_inc(s.y3_sb, 1)
                dve.wait_ge(s.y3_sb, upto(f))
                norm_stats(f, y3, st3, mv3, ve3, s.st3_sb, s.mv3_sb, s.ve3_sb)

            def x_yo(f):
                dve.wait_ge(s.rs3_sb, upto(f))
                dve.wait_ge(s.y_out, stored(f))
                ts(yo[:], y3[:], mv3[:, 0:1], rs3[:], ALU.subtract, ALU.mult).then_inc(s.yo_sb, 1)

            nc.vector.memset(bias3[:], 0.0)
            nc.vector.memset(Mp[:], 0.0).then_inc(s.bias_set, 1)
            nc.vector.memset(zeros[:], 0.0).then_inc(s.pads_set, 1)
            nc.vector.memset(ones_f[:], 1.0).then_inc(s.ones_set, 1)
            nc.vector.memset(ones_bf[:], 1.0).then_inc(s.ones_set, 1)
            dve.wait_ge(s.const_in, CONST_IN)
            dve.wait_ge(s.bias_set, 1)
            nc.vector.tensor_copy(bias3[0:1, :], bias_in[:]).then_inc(s.bias_step, 1)
            dve.wait_ge(s.bias_step, 1)
            tt(bias_rest[:], bias_in[:], bias3[0:1, :], ALU.subtract).then_inc(s.bias_step, 1)
            dve.wait_ge(s.bias_step, 2)
            nc.vector.tensor_copy(bias_mid[:], bias_rest[:]).then_inc(s.bias_step, 1)
            nc.vector.tensor_copy(bias3[32:33, :], bias_rest[:]).then_inc(s.bias_parts, 1)
            dve.wait_ge(s.bias_step, 3)
            tt(bias3[64:65, :], bias_rest[:], bias_mid[:], ALU.subtract).then_inc(s.bias_parts, 1)
            nw = NX * NR
            for c in range(CH):
                center = wx_sb[:, c, 2 * nw:NW]
                tt(wx_prod[:, c, 0:nw].rearrange("p (n r) -> p n r", r=NR),
                   wx_sb[:, c, 0:nw].rearrange("p (n r) -> p n r", r=NR),
                   center.unsqueeze(2).broadcast_to([P, NX, NR]), ALU.mult)
                last = tt(wx_prod[:, c, nw:2 * nw].rearrange("p (n r) -> p n r", r=NR),
                          wx_sb[:, c, nw:2 * nw].rearrange("p (n r) -> p n r", r=NR),
                          debias_sb[:, c, :].unsqueeze(2).broadcast_to([P, NX, NR]), ALU.mult)
            last.then_inc(s.prod_set, 1)
            tt(wx_prod[:, :, 2 * nw:NW], wx_sb[:, :, 2 * nw:NW], wx_sb[:, :, 2 * nw:NW],
               ALU.mult).then_inc(s.prod_set, 2)
            dve.wait_ge(s.shift_ps, 1)
            nc.vector.tensor_copy(wx_shift[:], bank[0][:, 0:NW]).then_inc(s.shift_set, 1)
            dve.wait_ge(s.shift_set, 1)

            def step(a):
                b, c, e, f = a.older(1), a.older(2), a.older(3), a.older(4)
                if b.real():
                    for j in range(4):
                        a_max(b, j)
                if e.real():
                    r_h(e)
                if c.real():
                    m_gs(c)
                if a.real():
                    p_q(a)
                if e.real():
                    r_var(e)
                if c.real():
                    m_logf(c)
                if a.real():
                    p_k(a)
                if c.real():
                    m_scan(c)
                if a.real():
                    p_T(a, 0)
                    p_VT(a)
                if b.real():
                    a_PT(b, 0)
                    a_PT(b, 1)
                if c.real():
                    m_acol(c)
                if f.real():
                    x_choose(f)
                if a.real():
                    p_T(a, 1)
                if f.real():
                    x_gate(f)
                if e.real():
                    r_r2(e)
                if b.real():
                    a_On(b)
                if e.real():
                    r_x2(e)
                if f.real():
                    x_LT(f)
                if c.real():
                    m_C(c, 0)
                if f.real():
                    x_y3(f)
                if c.real():
                    m_C(c, 1)
                    m_C(c, 2)
                if f.real():
                    x_yo(f)
                if b.real():
                    a_r1(b)
                if c.real():
                    m_C(c, 3)
                if b.real():
                    a_x1(b)

            def twice(tile):
                return 2 * (tile.k + 1) if tile.regs is None else tile.regs[("twice", tile.k + 1)]

            steps(dve, step)


def kernel(**inputs):
    import ml_dtypes
    import numpy as np
    import concourse.bacc as bacc
    from concourse.bass_utils import run_bass_kernel_spmd as run

    i = {n: np.ascontiguousarray(a) for n, a in inputs.items()}

    pair = np.arange(E).reshape(H, D // 2, 2).transpose(0, 2, 1).reshape(E)
    token = np.arange(P) % 32 * 4 + np.arange(P) // 32
    inv = (1.0 / 10000.0 ** (np.arange(0, D, 2, dtype=np.float32) / np.float32(D))).astype(np.float32)
    freq = (token.astype(np.float32)[:, None] * inv).astype(np.float32).astype(np.float64)
    cos, sin = np.cos(freq), np.sin(freq)
    cos2, sin2 = np.concatenate([cos, cos], 1), np.concatenate([-sin, sin], 1)
    scale = D ** -0.5
    rope = np.stack([cos2 * scale, sin2 * scale, cos2, sin2], 1).astype(np.float32)
    row_i, col_i = np.arange(P) % 8, np.arange(4 * P) % 8
    mask_l, mask_r = np.zeros((P, P)), np.zeros((P, 4 * P))
    for n in range(8):
        mask_l[n] = row_i == n
        mask_r[n] = np.where(col_i == n, 0.0, -1e30)
    head_rows = np.zeros((80, H, P))
    for h in range(H):
        head_rows[[h, 32 + h, 64 + h], h] = 1.0
    bf16 = ml_dtypes.bfloat16

    def flat(a):
        return a.transpose(1, 0, 2).reshape(E, NX * NR)

    arrays = {
        "x": i["x"], "ctx": i["ctx_2048"],
        "wq": i["L0_attn_Wq"][pair].T, "wk": i["L0_attn_Wk"][pair].T,
        "wv": i["L0_attn_Wv"].T, "wo": i["L0_attn_Wo"].T,
        "bqkv": np.concatenate([i["L0_attn_bq"][pair], i["L0_attn_bk"][pair], i["L0_attn_bv"]])[None],
        "bo": i["L0_attn_bo"][None],
        "rope": rope, "ident": np.eye(P, dtype=np.float32),
        "mask_l": mask_l.astype(bf16), "mask_r": mask_r.astype(bf16), "head_rows": head_rows.astype(bf16),
        "w_gate": np.concatenate([i["L0_xattn_Wi"], i["L0_xattn_Wf"]], 1),
        "b_gate": np.concatenate([i["L0_xattn_bi"], i["L0_xattn_bf"]])[None],
        "ln_scale": i["L0_xattn_ln_scale"][None],
        "w_expert": np.concatenate([flat(i["L0_ffn_select_weight"]), flat(i["L0_ffn_lora_update"]),
                                    i["L0_ffn_select_mean_diff"].T], 1),
        "debias": i["L0_ffn_debias_w"].T,
        "degen": np.concatenate([i["L0_ffn_lora_degen"].transpose(0, 2, 1).reshape(NX * NR, E),
                                 i["L0_ffn_bias_w"]]),
        "expert_rows": np.stack([i["L0_ffn_imp_center"], i["L0_ffn_imp_slope"],
                                 np.arange(NX, 0, -1, dtype=np.float32)]),
    }
    nc = bacc.Bacc("TRN2", target_bir_lowering=False, num_devices=1)
    args, ins = {}, {}
    for name, a in arrays.items():
        a = np.ascontiguousarray(a)
        ins[f"in_{name}"] = a
        args[name] = nc.dram_tensor(f"in_{name}", a.shape, mybir.dt.from_np(a.dtype), kind="ExternalInput").ap()
    out = nc.dram_tensor("out_dram", (NT, P, E), F32, kind="ExternalOutput").ap()
    bass_decoder(nc, out=out, **args)
    return run(nc, [ins], core_ids=[0]).results[0]["out_dram"]
```

```python
from collections import namedtuple
from contextlib import ExitStack

import concourse.bass as bass
from concourse import mybir

ALU = mybir.AluOpType
ACT = mybir.ActivationFunctionType
AX_X = mybir.AxisListType.X
F32 = mybir.dt.float32
BF16 = mybir.dt.bfloat16

P = 128
NT = 64
E = 512
CH = E // P
H = 16
D = E // H
HD = D + 1
G = 16
GW = 32 + H
NX = 8
NR = 8
NW = 2 * NX * NR + NX
NL = NX * NR + NX
LN_EPS = 1e-5
ML_EPS = 1e-6

LAGS = 4
QK_BANKS = 4, 7, 4, 7
PADS = 4
PEEL = 6


class Tile:

    def __init__(self, k, regs=None, dma=None, u=None):
        self.k, self.regs, self.dma, self.u = k, regs, dma, u

    def older(self, n):
        return Tile(self.k - n, self.regs, self.dma, self.u)

    def parity(self):
        return self.k % 2

    def real(self):
        return self.regs is not None or 0 <= self.k < NT

    def index(self):
        return self.k if self.u is None else self.u * 2 + self.k


def upto(tile, back=0):
    if tile.regs is None:
        return min(max(tile.k + 1 - back, 0), NT)
    return tile.regs[tile.k + 1 - back]


def upto_quarter(tile, j):
    if tile.regs is None:
        return 4 * tile.k + j + 1
    return tile.regs[("quarter", 4 * tile.k + j + 1)]


def landed(tile, pieces):
    if tile.dma is None:
        return 16 * pieces * (tile.k // 2 + 1)
    return tile.dma[(pieces, tile.k // 2 + 1)]


def stored(tile):
    return 16 * tile.k if tile.dma is None else tile.dma[("out", tile.k)]


def bass_decoder(nc, x, ctx, wq, wk, wv, wo, bqkv, bo, rope, ident, mask_l, mask_r, head_rows,
                 w_gate, b_gate, ln_scale, w_expert, debias, degen, expert_rows, out):
    with ExitStack() as stack:
        def sb(name, shape, dt=F32):
            return stack.enter_context(nc.sbuf_tensor(name, shape, dt))

        def sem(name):
            return stack.enter_context(nc.semaphore(name))

        w_sb = [sb(f"w{n}_sb", [P, CH, E]) for n in "qkvo"]
        bias_in = sb("bias_in", [1, 3 * E])
        bias3 = sb("bias3", [P, 3 * E], BF16)
        bias_rest = sb("bias_rest", [1, 3 * E])
        bias_mid = sb("bias_mid", [1, 3 * E], BF16)
        ones_bf = sb("ones_bf", [P, P], BF16)
        ones_f = sb("ones_f", [P, P])
        bo_sb = sb("bo_sb", [P, E])
        rope_sb = sb("rope_sb", [P, 4, D])
        id_sb = sb("id_sb", [P, P])
        mask_l_sb = sb("mask_l_sb", [P, P], BF16)
        mask_r_sb = sb("mask_r_sb", [P, 4 * P], BF16)
        head_sb = sb("head_sb", [80, H, P], BF16)
        wg_sb = sb("wg_sb", [P, 3, CH, GW])
        wg_ctx = sb("wg_ctx", [P, CH, GW])
        bg_sb = sb("bg_sb", [GW, 1])
        lns_sb = sb("lns_sb", [P, E])
        wx_sb = sb("wx_sb", [P, CH, NW])
        debias_sb = sb("debias_sb", [P, CH, NX])
        wx_prod = sb("wx_prod", [P, CH, NW])
        wx_shift = sb("wx_shift", [P, NW])
        degen_sb = sb("degen_sb", [NL, E])
        xrow_sb = sb("xrow_sb", [P, 3, NX])
        eps_ln = sb("eps_ln", [P, 1])
        half_neg = sb("half_neg", [P, H])
        zeros = sb("zeros", [H, P])

        xb = [sb(f"xb{i}", [P, E]) for i in range(2)]
        xr = [sb(f"xr{i}", [P, E]) for i in range(2)]
        xres = [sb(f"xres{i}", [P, E]) for i in range(2)]
        xT = sb("xT", [P, CH, P])
        rot = [[sb(f"rot{n}{i}", [P, E]) for i in range(2)] for n in "qk"]
        rsum = [sb(f"rsum{n}", [P, E]) for n in "qk"]
        QT = [sb(f"QT{i}", [P, CH, P]) for i in range(2)]
        KT = [sb(f"KT{i}", [P, CH, P]) for i in range(2)]
        VT = sb("VT", [P, CH, P])
        VG = [sb(f"VG{i}", [P, CH, P]) for i in range(2)]
        neg_max = sb("neg_max", [P, G])
        ex = sb("ex", [P, G, P])
        PT = sb("PT", [P, G, P])
        w_sum = sb("w_sum", [P, G])
        w_rec = sb("w_rec", [P, G])
        OT = sb("OT", [P, CH, P])
        r1 = sb("r1", [P, E])
        st1 = sb("st1", [P, 6])
        mv1 = sb("mv1", [P, 2])
        ve1 = sb("ve1", [P, 1])
        rs1 = sb("rs1", [P, 1])
        x1 = [sb(f"x1_{i}", [P, E]) for i in range(2)]
        cb = [sb(f"cb{i}", [P, E]) for i in range(2)]
        c1 = [sb(f"c1_{i}", [P, H, HD]) for i in range(2)]
        x1T = sb("x1T", [P, CH, P])
        cT = sb("cT", [P, CH, P])
        gs = sb("gs", [GW, P])
        g_abs = sb("g_abs", [GW, P])
        g_exp = sb("g_exp", [GW, P])
        g_ln = sb("g_ln", [GW, P])
        log_f = sb("log_f", [H, P])
        Fs = sb("Fs", [H, P])
        a_row = sb("a_row", [H, P])
        M_row = sb("M_row", [H, P])
        FM = sb("FM", [H, P])
        m_rest = sb("m_rest", [H, P])
        m_mid = sb("m_mid", [H, P], BF16)
        Mp = sb("Mp", [80, P], BF16)
        a_col = sb("a_col", [P, H])
        eFM = sb("eFM", [P, H])
        Dx = sb("Dx", [P, 4, CH, P])
        Cs = sb("Cs", [P, 4, CH, P])
        h_n0 = sb("h_n0", [P, H])
        h_n1 = sb("h_n1", [P, H])
        h_n2 = sb("h_n2", [P, H])
        h_rec = sb("h_rec", [P, H])
        hn = sb("hn", [P, H, D])
        h_sum = sb("h_sum", [P, H])
        cen = sb("cen", [P, H, D])
        cen2 = sb("cen2", [P, H, D])
        h_var = sb("h_var", [P, H])
        h_ve = sb("h_ve", [P, H])
        h_rs = sb("h_rs", [P, H])
        y1 = sb("y1", [P, H, D])
        y2 = sb("y2", [P, E])
        r2 = sb("r2", [P, E])
        st2 = sb("st2", [P, 6])
        mv2 = sb("mv2", [P, 2])
        ve2 = sb("ve2", [P, 1])
        rs2 = sb("rs2", [P, 1])
        x2 = [sb(f"x2_{i}", [P, E]) for i in range(2)]
        rs2sq = sb("rs2sq", [P, 1])
        x2sq = [sb(f"x2sq{i}", [P, 1]) for i in range(2)]
        x2T = sb("x2T", [P, CH, P])
        fz = sb("fz", [P, 2 * NX * NR])
        fz2 = sb("fz2", [P, NX, NR])
        f_sc = sb("f_sc", [P, NX])
        f_n1 = sb("f_n1", [P, NX])
        f_n2 = sb("f_n2", [P, NX])
        f_n3 = sb("f_n3", [P, NX])
        f_s = sb("f_s", [P, NX])
        f_u = sb("f_u", [P, NX])
        f_v = sb("f_v", [P, NX])
        f_e = sb("f_e", [P, NX])
        f_e1 = sb("f_e1", [P, NX])
        gate = sb("gate", [P, NX])
        g_max = sb("g_max", [P, 1])
        g_key = sb("g_key", [P, NX])
        g_kmax = sb("g_kmax", [P, 1])
        g_rest = sb("g_rest", [P, 1])
        L = sb("L", [P, NL])
        LT = sb("LT", [NL, P])
        y3 = sb("y3", [P, E])
        st3 = sb("st3", [P, 6])
        mv3 = sb("mv3", [P, 2])
        ve3 = sb("ve3", [P, 1])
        rs3 = sb("rs3", [P, 1])
        yo = sb("yo", [P, E])

        bank = [stack.enter_context(nc.psum_tensor(f"bank{i}", [P, 512], F32)) for i in range(8)]

        once = """const_in ones_set bias_step bias_parts bias_set prod_set shift_ps
            shift_set pads_set""".split()
        each = """xT_ps xT_sb q_ps k_ps v_ps q_rot k_rot q_sum k_sum QT_sb KT_sb VT_sb VG_ps VG_sb xres_sb
            max_sb rec_sb O_ps OT_sb proj_ps r1_sb st1_sb mv1_sb ve1_sb rs1_sb x1_sb
            x1T_ps x1T_sb cT_ps cT_sb c1_sb gate_ps gs_sb gabs_sb gexp_sb gln_sb logf_sb
            Fs_sb a_sb M_sb FM_sb Mhi_sb Mrest_sb Mmid2_sb Mp_sb aT_ps acol_sb eFM_sb
            hn0_sb hn1_sb hn2_sb hrec_sb hn_sb hsum_sb cen_sb cen2_sb hvar_sb hve_sb hrs_sb y1_sb y2_sb r2_sb
            st2_sb mv2_sb ve2_sb rs2_sb x2_sb rs2sq_sb
            x2T_ps x2T_sb F_ps fz_sb fz2_sb fn1_sb fn2_sb fn3_sb fs_sb fu_sb fv_sb fe_sb fe1_sb
            gate_sb gmax_sb gkey_sb gkmax_sb oh_sb L_sb LT_ps LT_sb Y_ps y3_sb st3_sb mv3_sb
            ve3_sb rs3_sb yo_sb""".split()
        four = "S_ps ex_sb exn_sb PT_ps PT_sb D_ps Dx_sb Dm_sb QK_ps C_sb".split()
        two = "H_ps x_in c_in r_in".split()
        semaphores = {n: sem(n) for n in once + each + ["y_out"]}
        semaphores |= {n: [sem(f"{n}{j}") for j in range(4)] for n in four}
        semaphores |= {n: [sem(f"{n}{j}") for j in range(2)] for n in two}
        s = namedtuple("Semaphores", semaphores)(**semaphores)

        consts = [
            *[(w_sb[n][:], w.rearrange("(c p) n -> p c n", p=P)) for n, w in enumerate((wq, wk, wv, wo))],
            (bias_in[:], bqkv), (bo_sb[:], bo.broadcast_to([P, E])), (rope_sb[:], rope), (id_sb[:], ident),
            (mask_l_sb[:], mask_l), (mask_r_sb[:], mask_r), (head_sb[:], head_rows),
            (wg_sb[:], w_gate.rearrange("(m c p) n -> p m c n", p=P, c=CH)), (bg_sb[:], b_gate),
            (lns_sb[:], ln_scale.broadcast_to([P, E])), (wx_sb[:], w_expert.rearrange("(c p) n -> p c n", p=P)),
            (debias_sb[:], debias.rearrange("(c p) n -> p c n", p=P)), (degen_sb[:], degen),
            (xrow_sb[:], expert_rows.unsqueeze(0).broadcast_to([P, 3, NX])),
        ]
        CONST_IN = 16 * len(consts)

        def steps(eng, step, quarters=()):
            for t in range(PEEL):
                step(Tile(t))
            with eng.Fori(PEEL // 2, NT // 2) as u:
                regs = {k: eng.snap(u * 2 + k) for k in range(-LAGS - 1, 3)}
                regs |= {("quarter", k): eng.snap(u * 8 + k) for k in quarters}
                dma = {(n, k): eng.snap(u * (16 * n) + 16 * n * k) for n in (1, 4) for k in range(-1, 2)}
                dma |= {("out", k): eng.snap(u * 32 + 16 * k) for k in range(-LAGS, -LAGS + 2)}
                for k in range(2):
                    step(Tile(k, regs, dma, u))
            for t in range(NT, NT + LAGS):
                step(Tile(t))

        x_v = x.rearrange("b (s q) e -> b q s e", q=4)
        block = stack.enter_context(nc.Block())

        @block.sync
        def _(sp):
            for dst, src in consts:
                sp.dma_start(dst, src).then_inc(s.const_in, 16)

            def load_x(t):
                for q in range(4):
                    sp.dma_start(xb[t.parity()][32 * q:32 * q + 32, :], x_v[t.index(), q]).then_inc(
                        s.x_in[t.parity()], 16)

            def load_res(t):
                sp.dma_start(xr[t.parity()][:], x[t.index()]).then_inc(s.r_in[t.parity()], 16)

            def load_ctx(t):
                sp.dma_start(cb[t.parity()][:], ctx[t.index()]).then_inc(s.c_in[t.parity()], 16)

            def store(t):
                sp.wait_ge(s.yo_sb, upto(t))
                sp.dma_start(out[t.index()], yo[:]).then_inc(s.y_out, 16)

            load_x(Tile(0))
            load_res(Tile(0))

            def step(a):
                nxt, c, f = a.older(-1), a.older(1), a.older(4)
                if nxt.real() and not (nxt.regs is None and nxt.k >= NT):
                    sp.wait_ge(s.xT_ps, upto(nxt, 2))
                    load_x(nxt)
                    sp.wait_ge(s.xres_sb, upto(nxt, 2))
                    load_res(nxt)
                if c.real():
                    sp.wait_ge(s.cT_ps, upto(c, 2))
                    sp.wait_ge(s.c1_sb, upto(c, 2))
                    load_ctx(c)
                if f.real():
                    store(f)

            for t in range(PEEL):
                step(Tile(t))
            with sp.Fori(PEEL // 2, NT // 2 - 1) as u:
                regs = {k: sp.snap(u * 2 + k) for k in range(-LAGS - 1, 3)}
                for k in range(2):
                    step(Tile(k, regs, None, u))
            for t in range(NT - 2, NT + LAGS):
                step(Tile(t))
            sp.wait_ge(s.y_out, 16 * NT)

        @block.tensor
        def _(pe):
            mm = nc.tensor.matmul

            def transposes(dst, src):
                for c in range(CH):
                    last = nc.tensor.transpose(dst[:, c * P:(c + 1) * P], src[:, c * P:(c + 1) * P], id_sb[:])
                return last

            def p_xT(a):
                pe.wait_ge(s.x_in[a.parity()], landed(a, 4))
                pe.wait_ge(s.C_sb[2], upto(a, 3))
                transposes(bank[4], xb[a.parity()]).then_inc(s.xT_ps, 1)

            def p_bias(n, b):
                mm(bank[b][:], ones_bf[:], bias3[:, n * E:(n + 1) * E], start=True, stop=False)

            def p_chunk(n, b, c):
                return mm(bank[b][:], xT[:, c, :], w_sb[n][:, c, :], start=False, stop=(c == CH - 1))

            def p_proj(a, n, b, out_sem):
                p_bias(n, b)
                for c in range(CH):
                    last = p_chunk(n, b, c)
                last.then_inc(out_sem, 1)

            def p_q_r_H(a, e):
                if a.real():
                    pe.wait_ge(s.xT_sb, upto(a))
                    pe.wait_ge(s.cT_sb, upto(a, 2))
                    p_bias(0, 6)
                if e.real():
                    for j in range(4):
                        pe.wait_ge(s.C_sb[j], upto(e))
                    pe.wait_ge(s.c1_sb, upto(e))
                for c in range(CH):
                    m = c // 2
                    if a.real():
                        last_q = p_chunk(0, 6, c)
                    if e.real():
                        if c == 2:
                            pe.wait_ge(s.xT_sb, upto(e, -3))
                        for h in range(4 * c, 4 * c + 4):
                            last_h = mm(bank[(7, 4)[m]][:, (h % 8) * HD:(h % 8 + 1) * HD], Cs[:, h % 4, h // 4, :],
                                        c1[e.parity()][:, h, :], start=True, stop=True)
                        if c % 2 == 1:
                            last_h.then_inc(s.H_ps[m], 1)
                if a.real():
                    last_q.then_inc(s.q_ps, 1)

            def p_k(a):
                pe.wait_ge(s.hn_sb, upto(a, 3))
                p_proj(a, 1, 4, s.k_ps)

            def p_v(a):
                pe.wait_ge(s.q_rot, upto(a))
                p_proj(a, 2, 6, s.v_ps)

            def p_VG(a):
                pe.wait_ge(s.VT_sb, upto(a))
                pe.wait_ge(s.k_rot, upto(a))
                for c in range(CH):
                    last = nc.tensor.transpose(bank[4][:, c * P:(c + 1) * P],
                                               VT[:, c, :], id_sb[:])
                last.then_inc(s.VG_ps, 1)

            def a_S(b):
                pe.wait_ge(s.QT_sb, upto(b))
                pe.wait_ge(s.KT_sb, upto(b))
                q_v, k_v = QT[b.parity()], KT[b.parity()]
                for j in range(4):
                    pe.wait_ge(s.Dx_sb[j], upto(b, 2))
                    mm(bank[j][:], mask_l_sb[:], mask_r_sb[:], start=True, stop=True, skip_group_check=True)
                    rows = slice(32 * j, 32 * j + 32)
                    for c in range(CH):
                        last = mm(bank[j][:, c * P:(c + 1) * P], q_v[rows, c, :], k_v[rows, c, :],
                                  start=False, stop=True, skip_group_check=True)
                    last.then_inc(s.S_ps[j], 1)

            def a_PT(b):
                for j in range(4):
                    pe.wait_ge(s.exn_sb[j], upto(b))
                    for c in range(CH):
                        last = nc.tensor.transpose(bank[j][:, c * P:(c + 1) * P], ex[:, 4 * j + c, :], id_sb[:])
                    last.then_inc(s.PT_ps[j], 1)

            def a_O(b):
                pe.wait_ge(s.VG_sb, upto(b))
                pe.wait_ge(s.VT_sb, upto(b, -1))
                for j in range(4):
                    pe.wait_ge(s.PT_sb[j], upto(b))
                    for c in range(CH):
                        last = mm(bank[6][32 * j:32 * j + 32, c * P:(c + 1) * P],
                                  VG[b.parity()][:, c, 32 * j:32 * j + 32], PT[:, 4 * j + c, :],
                                  start=True, stop=True, tile_position=(0, 32 * j))
                last.then_inc(s.O_ps, 1)

            def a_proj(b):
                pe.wait_ge(s.OT_sb, upto(b))
                pe.wait_ge(s.LT_sb, upto(b, 3))
                if b.regs is None:
                    pe.wait_ge(s.acol_sb, upto(b, 1))
                    pe.wait_ge(s.eFM_sb, upto(b, 1))
                for c in range(CH):
                    last = mm(bank[5][:], OT[:, c, :], w_sb[3][:, c, :], start=(c == 0), stop=(c == CH - 1))
                last.then_inc(s.proj_ps, 1)

            def m_T(c):
                pe.wait_ge(s.x1_sb, upto(c))
                pe.wait_ge(s.r1_sb, upto(c))
                transposes(bank[5], x1[c.parity()]).then_inc(s.x1T_ps, 1)
                pe.wait_ge(s.c_in[c.parity()], landed(c, 1))
                pe.wait_ge(s.y3_sb, upto(c, 3))
                transposes(bank[6], cb[c.parity()]).then_inc(s.cT_ps, 1)

            def m_gate(c):
                pe.wait_ge(s.x1T_sb, upto(c))
                pe.wait_ge(s.cT_sb, upto(c))
                for n in range(CH):
                    mm(bank[5][0:GW, 0:P], wg_sb[:, 0, n, :], x1T[:, n, :], start=(n == 0), stop=False)
                for n in range(CH):
                    last = mm(bank[5][0:GW, 0:P], wg_ctx[:, n, :], cT[:, n, :], start=False, stop=(n == CH - 1))
                last.then_inc(s.gate_ps, 1)

            def m_aT(c):
                pe.wait_ge(s.pads_set, PADS)
                pe.wait_ge(s.FM_sb, upto(c))
                nc.tensor.transpose(bank[5][:, 0:H], a_row[:], id_sb[0:H, 0:H])
                nc.tensor.transpose(bank[5][:, H:2 * H], FM[:], id_sb[0:H, 0:H]).then_inc(s.aT_ps, 1)

            def m_D(c):
                pe.wait_ge(s.Mp_sb, upto(c))
                pe.wait_ge(s.Mmid2_sb, upto(c))
                for j in range(4):
                    pe.wait_ge(s.PT_sb[j], upto(c, -1))
                    for n in range(CH):
                        last = mm(bank[j][:, n * P:(n + 1) * P], head_sb[:, 4 * n + j, :], Mp[:],
                                  start=True, stop=True)
                    last.then_inc(s.D_ps[j], 1)

            def m_QK(c, j):
                free = ((s.VG_sb, upto(c, -2)), (s.fn1_sb, upto(c, 2)), (s.C_sb[0], upto(c)), (s.C_sb[1], upto(c)))
                pe.wait_ge(*free[j])
                if j == 1 and c.regs is None:
                    pe.wait_ge(s.hn_sb, upto(c, 1))
                rows = slice(32 * j, 32 * j + 32)
                b = QK_BANKS[j]
                for n in range(CH):
                    last = mm(bank[b][:, n * P:(n + 1) * P], cT[rows, n, :], x1T[rows, n, :], start=True, stop=True)
                last.then_inc(s.QK_ps[j], 1)

            def x_x2T(f):
                pe.wait_ge(s.x2_sb, upto(f))
                pe.wait_ge(s.hn_sb, upto(f, -1))
                transposes(bank[7], x2[f.parity()]).then_inc(s.x2T_ps, 1)

            def x_F(f):
                pe.wait_ge(s.x2T_sb, upto(f))
                for c in range(CH):
                    last = mm(bank[7][:, 0:NW], x2T[:, c, :], wx_sb[:, c, :], start=(c == 0), stop=(c == CH - 1))
                last.then_inc(s.F_ps, 1)

            def x_LT(f):
                pe.wait_ge(s.L_sb, upto(f))
                pe.wait_ge(s.oh_sb, upto(f))
                pe.wait_ge(s.acol_sb, upto(f, -2))
                pe.wait_ge(s.eFM_sb, upto(f, -2))
                nc.tensor.transpose(bank[5][0:NL, 0:P], L[:], id_sb[:]).then_inc(s.LT_ps, 1)

            def x_Y(f):
                pe.wait_ge(s.LT_sb, upto(f))
                pe.wait_ge(s.OT_sb, upto(f, -3))
                mm(bank[6][:], LT[:], degen_sb[:], start=True, stop=True).then_inc(s.Y_ps, 1)

            def settle(a):
                pe.wait_ge(s.VG_sb, upto(a, 1))
                for j in range(4):
                    pe.wait_ge(s.Dx_sb[j], upto(a, 3))
                    pe.wait_ge(s.C_sb[j], upto(a, 3))
                pe.wait_ge(s.OT_sb, upto(a, 2))
                pe.wait_ge(s.fn1_sb, upto(a, 5))
                pe.wait_ge(s.y3_sb, upto(a, 5))

            pe.wait_ge(s.const_in, CONST_IN)
            pe.wait_ge(s.prod_set, 3)
            pe.wait_ge(s.ones_set, 2)
            for c in range(CH):
                last = mm(bank[0][:, 0:NW], ones_f[:], wx_prod[:, c, :], start=(c == 0), stop=(c == CH - 1))
            last.then_inc(s.shift_ps, 1)
            pe.wait_ge(s.shift_set, 1)
            pe.wait_ge(s.bias_set, 1)
            pe.wait_ge(s.bias_parts, 2)
            pe.wait_ge(s.pads_set, PADS)

            def step(a):
                b, c, e, f = a.older(1), a.older(2), a.older(3), a.older(4)
                if a.regs is None:
                    settle(a)
                if a.real():
                    p_xT(a)
                if b.real():
                    a_S(b)
                if c.real():
                    m_T(c)
                p_q_r_H(a, e)
                if c.real():
                    m_gate(c)
                if f.real():
                    x_x2T(f)
                if a.real():
                    p_k(a)
                if f.real():
                    x_F(f)
                if a.real():
                    p_v(a)
                if b.real():
                    a_PT(b)
                if c.real():
                    m_aT(c)
                if a.real():
                    p_VG(a)
                if b.real():
                    a_O(b)
                if f.real():
                    x_LT(f)
                if c.real():
                    m_D(c)
                    m_QK(c, 0)
                    m_QK(c, 1)
                if f.real():
                    x_Y(f)
                if c.real():
                    m_QK(c, 2)
                    m_QK(c, 3)
                if b.real():
                    a_proj(b)

            steps(pe, step)

        @block.scalar
        def _(act):
            def copy4(dst, b):
                return nc.scalar.activation(dst, bank[b][:], ACT.Copy)

            def p_xT(a):
                act.wait_ge(s.xT_ps, upto(a))
                act.wait_ge(s.v_ps, upto(a, 1))
                copy4(xT[:].rearrange("p c n -> p (c n)"), 4).then_inc(s.xT_sb, 1)

            def p_VG(a):
                act.wait_ge(s.VG_ps, upto(a))
                act.wait_ge(s.O_ps, upto(a, 2))
                copy4(VG[a.parity()][:].rearrange("p c n -> p (c n)"), 4).then_inc(s.VG_sb, 1)

            def a_exp(b, j):
                act.wait_ge(s.max_sb, upto_quarter(b, j))
                act.wait_ge(s.PT_ps[j], upto(b, 1))
                for c in range(CH):
                    g = 4 * j + c
                    last = nc.scalar.activation(ex[:, g, :], bank[j][:, c * P:(c + 1) * P], ACT.Exp,
                                                bias=neg_max[:, g:g + 1], accum_out=w_sum[:, g:g + 1])
                last.then_inc(s.ex_sb[j], 1)

            def a_PT(b, j):
                act.wait_ge(s.PT_ps[j], upto(b))
                act.wait_ge(s.O_ps, upto(b, 1))
                copy4(PT[:, 4 * j:4 * j + 4, :].rearrange("p g m -> p (g m)"), j).then_inc(s.PT_sb[j], 1)

            def a_OT(b):
                act.wait_ge(s.O_ps, upto(b))
                act.wait_ge(s.proj_ps, upto(b, 1))
                copy4(OT[:].rearrange("p c n -> p (c n)"), 6).then_inc(s.OT_sb, 1)

            def m_T(c):
                act.wait_ge(s.x1T_ps, upto(c))
                act.wait_ge(s.QK_ps[3], upto(c, 1))
                copy4(x1T[:].rearrange("p c n -> p (c n)"), 5).then_inc(s.x1T_sb, 1)
                act.wait_ge(s.cT_ps, upto(c))
                copy4(cT[:].rearrange("p c n -> p (c n)"), 6).then_inc(s.cT_sb, 1)

            def m_gate(c):
                act.wait_ge(s.gabs_sb, upto(c))
                nc.scalar.activation(g_exp[32:GW, :], g_abs[32:GW, :], ACT.Exp).then_inc(s.gexp_sb, 1)
                act.wait_ge(s.gexp_sb, upto(c))
                nc.scalar.activation(g_ln[32:GW, :], g_exp[32:GW, :], ACT.Ln, bias=1.0).then_inc(s.gln_sb, 1)

            def m_eFM(c):
                act.wait_ge(s.acol_sb, upto(c))
                act.wait_ge(s.hn1_sb, upto(c, 1))
                nc.scalar.activation(eFM[:], bank[5][:, H:2 * H], ACT.Exp, scale=-1.0).then_inc(s.eFM_sb, 1)

            def m_Dx(c, j):
                act.wait_ge(s.D_ps[j], upto(c))
                act.wait_ge(s.acol_sb, upto(c))
                act.wait_ge(s.C_sb[j], upto(c, 1))
                for n in range(CH):
                    h = 4 * n + j
                    last = nc.scalar.activation(Dx[:, j, n, :], bank[j][:, n * P:(n + 1) * P], ACT.Exp,
                                                bias=a_col[:, h:h + 1])
                last.then_inc(s.Dx_sb[j], 1)

            def r_sq(e):
                act.wait_ge(s.cen_sb, upto(e))
                act.wait_ge(s.hvar_sb, upto(e, 1))
                nc.scalar.activation(cen2[:], cen[:], ACT.Square).then_inc(s.cen2_sb, 1)

            def x_x2T(f):
                act.wait_ge(s.x2T_ps, upto(f))
                act.wait_ge(s.F_ps, upto(f, 1))
                copy4(x2T[:].rearrange("p c n -> p (c n)"), 7).then_inc(s.x2T_sb, 1)

            def x_exp(f):
                act.wait_ge(s.fv_sb, upto(f))
                act.wait_ge(s.fe1_sb, upto(f, 1))
                nc.scalar.activation(f_e[:], f_v[:], ACT.Exp, scale=-1.0).then_inc(s.fe_sb, 1)

            nc.scalar.preload_act_table_set("natural_log_exp_and_others")
            act.wait_ge(s.const_in, CONST_IN)

            def step(a):
                b, c, e, f = a.older(1), a.older(2), a.older(3), a.older(4)
                if a.real():
                    p_xT(a)
                if b.real():
                    a_exp(b, 0)
                if c.real():
                    m_T(c)
                if b.real():
                    a_exp(b, 1)
                    a_exp(b, 2)
                    a_exp(b, 3)
                if c.real():
                    m_gate(c)
                if e.real():
                    r_sq(e)
                if f.real():
                    x_x2T(f)
                if b.real():
                    a_PT(b, 2)
                    a_PT(b, 3)
                if f.real():
                    x_exp(f)
                if c.real():
                    m_eFM(c)
                if a.real():
                    p_VG(a)
                if b.real():
                    a_OT(b)
                if c.real():
                    for j in range(4):
                        m_Dx(c, j)

            steps(act, step, range(-3, 5))

        @block.gpsimd
        def _(pool):
            tt = nc.gpsimd.tensor_tensor

            def p_xres(a):
                pool.wait_ge(s.r_in[a.parity()], landed(a, 1))
                pool.wait_ge(s.r1_sb, upto(a, 2))
                tt(xres[a.parity()][:], xr[a.parity()][:], bo_sb[:], ALU.add).then_inc(s.xres_sb, 1)

            def p_rot(a, n):
                pool.wait_ge((s.q_rot, s.k_rot)[n], upto(a))
                pool.wait_ge((s.QT_sb, s.KT_sb)[n], upto(a, 1))
                tt(rsum[n][:], rot[n][0][:], rot[n][1][:], ALU.add).then_inc((s.q_sum, s.k_sum)[n], 1)

            def m_c1(c):
                pool.wait_ge(s.c_in[c.parity()], landed(c, 1))
                pool.wait_ge(s.H_ps[1], upto(c, 2))
                tt(c1[c.parity()][:, :, 0:D], cb[c.parity()][:].rearrange("p (h d) -> p h d", d=D),
                   ones_f[:, 0:1].unsqueeze(2).broadcast_to([P, H, D]), ALU.mult).then_inc(s.c1_sb, 1)

            def a_scale(b, j):
                pool.wait_ge(s.rec_sb, upto_quarter(b, j))
                tt(ex[:, 4 * j:4 * j + 4, :], ex[:, 4 * j:4 * j + 4, :],
                   w_rec[:, 4 * j:4 * j + 4].unsqueeze(2).broadcast_to([P, 4, P]), ALU.mult).then_inc(s.exn_sb[j], 1)

            def m_mask(c, j):
                pool.wait_ge(s.pads_set, PADS)
                pool.wait_ge(s.Dx_sb[j], upto(c))
                nc.gpsimd.affine_select(Dx[:, j], Dx[:, j], compare_op=ALU.is_ge, fill=0.0, base=0,
                                        pattern=[[0, CH], [1, P]],
                                        channel_multiplier=-1).then_inc(s.Dm_sb[j], 1)

            def r_head(e):
                pool.wait_ge(s.hve_sb, upto(e))
                pool.wait_ge(s.y1_sb, upto(e, 1))
                tt(h_rs[:], h_ve[:], half_neg[:], ALU.pow).then_inc(s.hrs_sb, 1)
                pool.wait_ge(s.hrs_sb, upto(e))
                pool.wait_ge(s.cen_sb, upto(e))
                pool.wait_ge(s.y2_sb, upto(e, 1))
                tt(y1[:], cen[:], h_rs[:].unsqueeze(2).broadcast_to([P, H, D]), ALU.mult).then_inc(s.y1_sb, 1)
                pool.wait_ge(s.y1_sb, upto(e))
                pool.wait_ge(s.r2_sb, upto(e, 1))
                tt(y2[:], y1[:].rearrange("p h d -> p (h d)"), lns_sb[:], ALU.mult).then_inc(s.y2_sb, 1)
                pool.wait_ge(s.y2_sb, upto(e))
                pool.wait_ge(s.x1_sb, upto(e))
                pool.wait_ge(s.x2_sb, upto(e, 1))
                tt(r2[:], y2[:], x1[e.parity()][:], ALU.add).then_inc(s.r2_sb, 1)

            def rsqrt(t, ve, rs, ve_sem, rs_sem, used):
                pool.wait_ge(ve_sem, upto(t))
                pool.wait_ge(used, upto(t, 1))
                tt(rs[:], ve[:], half_neg[:, 0:1], ALU.pow).then_inc(rs_sem, 1)

            pool.wait_ge(s.const_in, CONST_IN)
            nc.gpsimd.memset(half_neg[:], -0.5).then_inc(s.pads_set, 1)
            for i in range(2):
                last = nc.gpsimd.memset(c1[i][:], 1.0)
            last.then_inc(s.pads_set, 1)
            tt(wg_ctx[:], wg_sb[:, 1], wg_sb[:, 2], ALU.add).then_inc(s.pads_set, 1)
            pool.wait_ge(s.pads_set, PADS)
            pool.wait_ge(s.ones_set, 2)

            def step(a):
                b, c, e, f = a.older(1), a.older(2), a.older(3), a.older(4)
                if a.real():
                    p_xres(a)
                if c.real():
                    m_c1(c)
                if b.real():
                    for j in range(4):
                        a_scale(b, j)
                if a.real():
                    p_rot(a, 0)
                if e.real():
                    r_head(e)
                if a.real():
                    p_rot(a, 1)
                if e.real():
                    rsqrt(e, ve2, rs2, s.ve2_sb, s.rs2_sb, s.x2_sb)
                if c.real():
                    m_mask(c, 0)
                    m_mask(c, 1)
                if f.real():
                    rsqrt(f, ve3, rs3, s.ve3_sb, s.rs3_sb, s.yo_sb)
                if c.real():
                    m_mask(c, 2)
                    m_mask(c, 3)
                if b.real():
                    rsqrt(b, ve1, rs1, s.ve1_sb, s.rs1_sb, s.x1_sb)

            steps(pool, step, range(-3, 5))

        @block.vector
        def _(dve):
            tt = nc.vector.tensor_tensor
            ts = nc.vector.tensor_scalar
            stt = nc.vector.scalar_tensor_tensor
            red = nc.vector.tensor_reduce

            def rotate(t, n, b, ps, done, summed):
                dve.wait_ge(ps, upto(t))
                dve.wait_ge(summed, upto(t, 1))
                src = bank[b][:].rearrange("p (h d) -> p h d", d=D)
                cos = rope_sb[:, 2 * n, :].unsqueeze(1).broadcast_to([P, H, D])
                sin = rope_sb[:, 2 * n + 1, :].unsqueeze(1).broadcast_to([P, H, D])
                tt(rot[n][0][:].rearrange("p (h d) -> p h d", d=D), src, cos, ALU.mult)
                other = rot[n][1][:].rearrange("p (h d) -> p h d", d=D)
                tt(other[:, :, 0:D // 2], src[:, :, D // 2:D], sin[:, :, 0:D // 2], ALU.mult)
                tt(other[:, :, D // 2:D], src[:, :, 0:D // 2], sin[:, :, D // 2:D], ALU.mult).then_inc(done, 1)

            def p_q(a):
                rotate(a, 0, 6, s.q_ps, s.q_rot, s.q_sum)

            def p_k(a):
                rotate(a, 1, 4, s.k_ps, s.k_rot, s.k_sum)

            def by_group(t):
                return t[:].rearrange("p c (h i) -> p h i c", i=8)

            def p_T(a, n):
                dve.wait_ge((s.q_sum, s.k_sum)[n], upto(a))
                dve.wait_ge(s.S_ps[3], upto(a, 2))
                nc.vector.transpose(by_group((QT, KT)[n][a.parity()]), rsum[n][:]).then_inc((s.QT_sb, s.KT_sb)[n], 1)

            def p_VT(a):
                dve.wait_ge(s.v_ps, upto(a))
                dve.wait_ge(s.VG_ps, upto(a, 1))
                nc.vector.transpose(by_group(VT), bank[6][:]).then_inc(s.VT_sb, 1)

            def a_max(b, j):
                dve.wait_ge(s.S_ps[j], upto(b))
                dve.wait_ge(s.ex_sb[j], upto(b, 1))
                red(neg_max[:, 4 * j:4 * j + 4], bank[j][:].rearrange("p (g n) -> p g n", n=P), AX_X, ALU.max,
                    negate=True).then_inc(s.max_sb, 1)

            def a_rec(b, j):
                dve.wait_ge(s.ex_sb[j], upto(b))
                nc.vector.reciprocal(w_rec[:, 4 * j:4 * j + 4], w_sum[:, 4 * j:4 * j + 4]).then_inc(s.rec_sb, 1)

            def a_PT(b, j):
                dve.wait_ge(s.PT_ps[j], upto(b))
                dve.wait_ge(s.O_ps, upto(b, 1))
                nc.vector.tensor_copy(PT[:, 4 * j:4 * j + 4, :].rearrange("p g m -> p (g m)"),
                                      bank[j][:]).then_inc(s.PT_sb[j], 1)

            def norm_stats(t, r, st, mv, ve, st_sem, mv_sem, ve_sem):
                nc.vector.bn_stats(st[:], r[:]).then_inc(st_sem, 1)
                dve.wait_ge(s.pads_set, PADS)
                dve.wait_ge(st_sem, upto(t))
                nc.vector.bn_aggr(mv[:], st[:]).then_inc(mv_sem, 1)
                dve.wait_ge(mv_sem, upto(t))
                ts(ve[:], mv[:, 1:2], LN_EPS, None, ALU.add).then_inc(ve_sem, 1)

            def a_r1(b):
                dve.wait_ge(s.proj_ps, upto(b))
                dve.wait_ge(s.xres_sb, upto(b))
                tt(r1[:], bank[5][:], xres[b.parity()][:], ALU.add).then_inc(s.r1_sb, 1)
                dve.wait_ge(s.r1_sb, upto(b))
                norm_stats(b, r1, st1, mv1, ve1, s.st1_sb, s.mv1_sb, s.ve1_sb)

            def a_x1(b):
                dve.wait_ge(s.rs1_sb, upto(b))
                dve.wait_ge(s.r2_sb, upto(b, 2))
                ts(x1[b.parity()][:], r1[:], mv1[:, 0:1], rs1[:], ALU.subtract, ALU.mult).then_inc(s.x1_sb, 1)

            def m_gs(c):
                dve.wait_ge(s.gate_ps, upto(c))
                ts(gs[:], bank[5][0:GW, 0:P], bg_sb[:], None, ALU.add).then_inc(s.gs_sb, 1)
                dve.wait_ge(s.gs_sb, upto(c))
                stt(out=g_abs[32:GW, :], in0=gs[32:GW, :], scalar=-1.0, in1=gs[32:GW, :], op0=ALU.mult,
                    op1=ALU.min).then_inc(s.gabs_sb, 1)

            def m_logf(c):
                dve.wait_ge(s.gln_sb, upto(c))
                stt(out=log_f[:], in0=gs[32:GW, :], scalar=0.0, in1=g_ln[32:GW, :], op0=ALU.min,
                    op1=ALU.subtract).then_inc(s.logf_sb, 1)

            def m_scan(c):
                dve.wait_ge(s.logf_sb, upto(c))
                dve.wait_ge(s.aT_ps, upto(c, 1))
                dve.wait_ge(s.pads_set, PADS)
                nc.vector.tensor_tensor_scan(Fs[:], log_f[:], zeros[:], 0.0, ALU.add,
                                             ALU.add).then_inc(s.Fs_sb, 1)
                dve.wait_ge(s.Fs_sb, upto(c))
                tt(a_row[:], gs[0:H, :], Fs[:], ALU.subtract).then_inc(s.a_sb, 1)
                dve.wait_ge(s.a_sb, upto(c))
                nc.vector.tensor_tensor_scan(M_row[:], a_row[:], a_row[:], -3.0e38, ALU.max,
                                             ALU.max).then_inc(s.M_sb, 1)
                dve.wait_ge(s.M_sb, upto(c))
                tt(FM[:], Fs[:], M_row[:], ALU.add).then_inc(s.FM_sb, 1)
                dve.wait_ge(s.D_ps[3], upto(c, 1))
                ts(Mp[0:H, :], M_row[:], -1.0, None, ALU.mult).then_inc(s.Mhi_sb, 1)
                dve.wait_ge(s.Mhi_sb, upto(c))
                stt(out=m_rest[:], in0=M_row[:], scalar=-1.0, in1=Mp[0:H, :], op0=ALU.mult,
                    op1=ALU.subtract).then_inc(s.Mrest_sb, 1)
                dve.wait_ge(s.Mrest_sb, upto(c))
                nc.vector.tensor_copy(m_mid[:], m_rest[:])
                nc.vector.tensor_copy(Mp[32:32 + H, :], m_rest[:]).then_inc(s.Mmid2_sb, 1)
                dve.wait_ge(s.Mmid2_sb, upto(c))
                tt(Mp[64:64 + H, :], m_rest[:], m_mid[:], ALU.subtract).then_inc(s.Mp_sb, 1)

            def m_acol(c):
                dve.wait_ge(s.aT_ps, upto(c))
                dve.wait_ge(s.Dx_sb[3], upto(c, 1))
                nc.vector.tensor_copy(a_col[:], bank[5][:, 0:H]).then_inc(s.acol_sb, 1)

            def m_C(c, j):
                dve.wait_ge(s.QK_ps[j], upto(c))
                dve.wait_ge(s.Dm_sb[j], upto(c))
                dve.wait_ge(s.H_ps[1], upto(c, 1))
                stt(out=Cs[:, j], in0=bank[QK_BANKS[j]][:].rearrange("p (c n) -> p c n", n=P),
                    scalar=float(D) ** -0.5, in1=Dx[:, j], op0=ALU.mult, op1=ALU.mult).then_inc(s.C_sb[j], 1)

            def r_h(e):
                dve.wait_ge(s.eFM_sb, upto(e))
                for m in range(2):
                    dve.wait_ge(s.H_ps[m], upto(e))
                    hs = bank[(7, 4)[m]][:, 0:8 * HD].rearrange("p (h d) -> p h d", d=HD)
                    last = stt(out=h_n0[:, 8 * m:8 * m + 8], in0=hs[:, :, D], scalar=-1.0,
                               in1=eFM[:, 8 * m:8 * m + 8], op0=ALU.mult, op1=ALU.max)
                last.then_inc(s.hn0_sb, 1)
                dve.wait_ge(s.hn0_sb, upto(e))
                for m in range(2):
                    hs = bank[(7, 4)[m]][:, 0:8 * HD].rearrange("p (h d) -> p h d", d=HD)
                    last = tt(h_n1[:, 8 * m:8 * m + 8], hs[:, :, D], h_n0[:, 8 * m:8 * m + 8], ALU.max)
                last.then_inc(s.hn1_sb, 1)
                dve.wait_ge(s.hn1_sb, upto(e))
                ts(h_n2[:], h_n1[:], ML_EPS, None, ALU.add).then_inc(s.hn2_sb, 1)
                dve.wait_ge(s.hn2_sb, upto(e))
                nc.vector.reciprocal(h_rec[:], h_n2[:]).then_inc(s.hrec_sb, 1)
                dve.wait_ge(s.hrec_sb, upto(e))
                for m in range(2):
                    hs = bank[(7, 4)[m]][:, 0:8 * HD].rearrange("p (h d) -> p h d", d=HD)
                    last = tt(hn[:, 8 * m:8 * m + 8, :], hs[:, :, 0:D],
                              h_rec[:, 8 * m:8 * m + 8].unsqueeze(2).broadcast_to([P, 8, D]), ALU.mult)
                last.then_inc(s.hn_sb, 1)
                dve.wait_ge(s.hn_sb, upto(e))
                red(h_sum[:], hn[:], AX_X, ALU.add).then_inc(s.hsum_sb, 1)
                dve.wait_ge(s.hsum_sb, upto(e))
                dve.wait_ge(s.y1_sb, upto(e, 1))
                stt(out=cen[:], in0=h_sum[:].unsqueeze(2).broadcast_to([P, H, D]), scalar=-1.0 / D, in1=hn[:],
                    op0=ALU.mult, op1=ALU.add).then_inc(s.cen_sb, 1)

            def r_var(e):
                dve.wait_ge(s.cen2_sb, upto(e))
                red(h_var[:], cen2[:], AX_X, ALU.add).then_inc(s.hvar_sb, 1)
                dve.wait_ge(s.hvar_sb, upto(e))
                dve.wait_ge(s.hrs_sb, upto(e, 1))
                ts(h_ve[:], h_var[:], 1.0 / D, ML_EPS, ALU.mult, ALU.add).then_inc(s.hve_sb, 1)

            def r_r2(e):
                dve.wait_ge(s.r2_sb, upto(e))
                norm_stats(e, r2, st2, mv2, ve2, s.st2_sb, s.mv2_sb, s.ve2_sb)

            def r_x2(e):
                dve.wait_ge(s.rs2_sb, upto(e))
                tt(rs2sq[:], rs2[:], rs2[:], ALU.mult).then_inc(s.rs2sq_sb, 1)
                dve.wait_ge(s.rs2sq_sb, upto(e))
                ts(x2sq[e.parity()][:], mv2[:, 1:2], rs2sq[:], float(E), ALU.mult, ALU.mult)
                dve.wait_ge(s.x2T_ps, upto(e, 2))
                ts(x2[e.parity()][:], r2[:], mv2[:, 0:1], rs2[:], ALU.subtract, ALU.mult).then_inc(s.x2_sb, 1)

            def x_choose(f):
                dve.wait_ge(s.F_ps, upto(f))
                nw = NX * NR
                tt(fz[:], bank[7][:, 0:2 * nw], wx_shift[:, 0:2 * nw], ALU.subtract).then_inc(s.fz_sb, 1)
                stt(out=f_n1[:], in0=bank[7][:, 2 * nw:NW], scalar=-2.0, in1=wx_shift[:, 2 * nw:NW],
                    op0=ALU.mult, op1=ALU.add).then_inc(s.fn1_sb, 1)
                dve.wait_ge(s.fz_sb, upto(f))
                tt(fz2[:], fz[:, 0:nw].rearrange("p (n r) -> p n r", r=NR),
                   fz[:, 0:nw].rearrange("p (n r) -> p n r", r=NR), ALU.mult).then_inc(s.fz2_sb, 1)
                dve.wait_ge(s.fn1_sb, upto(f))
                dve.wait_ge(s.x2_sb, upto(f))
                ts(f_n2[:], f_n1[:], x2sq[f.parity()][:], None, ALU.add).then_inc(s.fn2_sb, 1)
                dve.wait_ge(s.fz2_sb, upto(f))
                red(f_sc[:], fz2[:], AX_X, ALU.add)
                dve.wait_ge(s.fn2_sb, upto(f))
                nc.vector.reciprocal(f_n3[:], f_n2[:]).then_inc(s.fn3_sb, 1)
                dve.wait_ge(s.fn3_sb, upto(f))
                tt(f_s[:], f_sc[:], f_n3[:], ALU.mult).then_inc(s.fs_sb, 1)
                dve.wait_ge(s.fs_sb, upto(f))
                tt(f_u[:], f_s[:], xrow_sb[:, 0, :], ALU.subtract).then_inc(s.fu_sb, 1)
                dve.wait_ge(s.fu_sb, upto(f))
                tt(f_v[:], f_u[:], xrow_sb[:, 1, :], ALU.mult).then_inc(s.fv_sb, 1)

            def x_gate(f):
                dve.wait_ge(s.fe_sb, upto(f))
                ts(f_e1[:], f_e[:], 1.0, None, ALU.add).then_inc(s.fe1_sb, 1)
                dve.wait_ge(s.fe1_sb, upto(f))
                nc.vector.reciprocal(gate[:], f_e1[:]).then_inc(s.gate_sb, 1)
                dve.wait_ge(s.gate_sb, upto(f))
                red(g_max[:], gate[:], AX_X, ALU.max).then_inc(s.gmax_sb, 1)
                dve.wait_ge(s.gmax_sb, upto(f))
                stt(out=g_key[:], in0=gate[:], scalar=g_max[:], in1=xrow_sb[:, 2, :], op0=ALU.is_equal,
                    op1=ALU.mult).then_inc(s.gkey_sb, 1)
                ts(g_rest[:], g_max[:], -1.0, 2.0, ALU.mult, ALU.add)
                dve.wait_ge(s.gkey_sb, upto(f))
                red(g_kmax[:], g_key[:], AX_X, ALU.max).then_inc(s.gkmax_sb, 1)
                dve.wait_ge(s.gkmax_sb, upto(f))
                dve.wait_ge(s.LT_ps, upto(f, 1))
                ts(L[:, NX * NR:NL], g_key[:], g_kmax[:], g_max[:], ALU.is_equal, ALU.mult).then_inc(s.oh_sb, 1)
                dve.wait_ge(s.oh_sb, upto(f))
                tt(L[:, 0:NX * NR].rearrange("p (n r) -> p n r", r=NR),
                   fz[:, NX * NR:2 * NX * NR].rearrange("p (n r) -> p n r", r=NR),
                   L[:, NX * NR:NL].unsqueeze(2).broadcast_to([P, NX, NR]), ALU.mult).then_inc(s.L_sb, 1)

            def x_LT(f):
                dve.wait_ge(s.LT_ps, upto(f))
                dve.wait_ge(s.Y_ps, upto(f, 1))
                nc.vector.tensor_copy(LT[:], bank[5][0:NL, 0:P]).then_inc(s.LT_sb, 1)

            def x_y3(f):
                dve.wait_ge(s.Y_ps, upto(f))
                dve.wait_ge(s.x2_sb, upto(f))
                stt(out=y3[:], in0=x2[f.parity()][:], scalar=g_rest[:], in1=bank[6][:], op0=ALU.mult,
                    op1=ALU.add).then_inc(s.y3_sb, 1)
                dve.wait_ge(s.y3_sb, upto(f))
                norm_stats(f, y3, st3, mv3, ve3, s.st3_sb, s.mv3_sb, s.ve3_sb)

            def x_yo(f):
                dve.wait_ge(s.rs3_sb, upto(f))
                dve.wait_ge(s.y_out, stored(f))
                ts(yo[:], y3[:], mv3[:, 0:1], rs3[:], ALU.subtract, ALU.mult).then_inc(s.yo_sb, 1)

            nc.vector.memset(bias3[:], 0.0)
            nc.vector.memset(Mp[:], 0.0).then_inc(s.bias_set, 1)
            nc.vector.memset(zeros[:], 0.0).then_inc(s.pads_set, 1)
            nc.vector.memset(ones_f[:], 1.0).then_inc(s.ones_set, 1)
            nc.vector.memset(ones_bf[:], 1.0).then_inc(s.ones_set, 1)
            dve.wait_ge(s.const_in, CONST_IN)
            dve.wait_ge(s.bias_set, 1)
            nc.vector.tensor_copy(bias3[0:1, :], bias_in[:]).then_inc(s.bias_step, 1)
            dve.wait_ge(s.bias_step, 1)
            tt(bias_rest[:], bias_in[:], bias3[0:1, :], ALU.subtract).then_inc(s.bias_step, 1)
            dve.wait_ge(s.bias_step, 2)
            nc.vector.tensor_copy(bias_mid[:], bias_rest[:]).then_inc(s.bias_step, 1)
            nc.vector.tensor_copy(bias3[32:33, :], bias_rest[:]).then_inc(s.bias_parts, 1)
            dve.wait_ge(s.bias_step, 3)
            tt(bias3[64:65, :], bias_rest[:], bias_mid[:], ALU.subtract).then_inc(s.bias_parts, 1)
            nw = NX * NR
            for c in range(CH):
                center = wx_sb[:, c, 2 * nw:NW]
                tt(wx_prod[:, c, 0:nw].rearrange("p (n r) -> p n r", r=NR),
                   wx_sb[:, c, 0:nw].rearrange("p (n r) -> p n r", r=NR),
                   center.unsqueeze(2).broadcast_to([P, NX, NR]), ALU.mult)
                last = tt(wx_prod[:, c, nw:2 * nw].rearrange("p (n r) -> p n r", r=NR),
                          wx_sb[:, c, nw:2 * nw].rearrange("p (n r) -> p n r", r=NR),
                          debias_sb[:, c, :].unsqueeze(2).broadcast_to([P, NX, NR]), ALU.mult)
            last.then_inc(s.prod_set, 1)
            tt(wx_prod[:, :, 2 * nw:NW], wx_sb[:, :, 2 * nw:NW], wx_sb[:, :, 2 * nw:NW],
               ALU.mult).then_inc(s.prod_set, 2)
            dve.wait_ge(s.shift_ps, 1)
            nc.vector.tensor_copy(wx_shift[:], bank[0][:, 0:NW]).then_inc(s.shift_set, 1)
            dve.wait_ge(s.shift_set, 1)

            def step(a):
                b, c, e, f = a.older(1), a.older(2), a.older(3), a.older(4)
                if b.real():
                    for j in range(4):
                        a_max(b, j)
                    for j in range(4):
                        a_rec(b, j)
                if a.real():
                    p_q(a)
                if e.real():
                    r_h(e)
                if c.real():
                    m_gs(c)
                if e.real():
                    r_var(e)
                if c.real():
                    m_logf(c)
                    m_scan(c)
                if a.real():
                    p_T(a, 0)
                    p_k(a)
                if f.real():
                    x_choose(f)
                if a.real():
                    p_VT(a)
                if f.real():
                    x_gate(f)
                if b.real():
                    a_PT(b, 0)
                    a_PT(b, 1)
                if c.real():
                    m_acol(c)
                if a.real():
                    p_T(a, 1)
                if f.real():
                    x_LT(f)
                if e.real():
                    r_r2(e)
                if c.real():
                    m_C(c, 0)
                if e.real():
                    r_x2(e)
                if c.real():
                    m_C(c, 1)
                if f.real():
                    x_y3(f)
                if c.real():
                    m_C(c, 2)
                if f.real():
                    x_yo(f)
                if c.real():
                    m_C(c, 3)
                if b.real():
                    a_r1(b)
                    a_x1(b)

            steps(dve, step)


def kernel(**inputs):
    import ml_dtypes
    import numpy as np
    import concourse.bacc as bacc
    from concourse.bass_utils import run_bass_kernel_spmd as run

    i = {n: np.ascontiguousarray(a) for n, a in inputs.items()}

    pair = np.arange(E).reshape(H, D // 2, 2).transpose(0, 2, 1).reshape(E)
    token = np.arange(P) % 32 * 4 + np.arange(P) // 32
    inv = (1.0 / 10000.0 ** (np.arange(0, D, 2, dtype=np.float32) / np.float32(D))).astype(np.float32)
    freq = (token.astype(np.float32)[:, None] * inv).astype(np.float32).astype(np.float64)
    cos, sin = np.cos(freq), np.sin(freq)
    cos2, sin2 = np.concatenate([cos, cos], 1), np.concatenate([-sin, sin], 1)
    scale = D ** -0.5
    rope = np.stack([cos2 * scale, sin2 * scale, cos2, sin2], 1).astype(np.float32)
    row_i, col_i = np.arange(P) % 8, np.arange(4 * P) % 8
    mask_l, mask_r = np.zeros((P, P)), np.zeros((P, 4 * P))
    for n in range(8):
        mask_l[n] = row_i == n
        mask_r[n] = np.where(col_i == n, 0.0, -1e30)
    head_rows = np.zeros((80, H, P))
    for h in range(H):
        head_rows[[h, 32 + h, 64 + h], h] = 1.0
    bf16 = ml_dtypes.bfloat16

    def flat(a):
        return a.transpose(1, 0, 2).reshape(E, NX * NR)

    def gate_rows(a_i, a_f):
        rows = np.zeros((GW, a_i.shape[1]), a_i.dtype)
        rows[0:H], rows[32:GW] = a_i, a_f
        return rows

    arrays = {
        "x": i["x"], "ctx": i["ctx_2048"],
        "wq": i["L0_attn_Wq"][pair].T, "wk": i["L0_attn_Wk"][pair].T,
        "wv": i["L0_attn_Wv"].T, "wo": i["L0_attn_Wo"].T,
        "bqkv": np.concatenate([i["L0_attn_bq"][pair], i["L0_attn_bk"][pair], i["L0_attn_bv"]])[None],
        "bo": i["L0_attn_bo"][None],
        "rope": rope, "ident": np.eye(P, dtype=np.float32),
        "mask_l": mask_l.astype(bf16), "mask_r": mask_r.astype(bf16), "head_rows": head_rows.astype(bf16),
        "w_gate": gate_rows(i["L0_xattn_Wi"].T, i["L0_xattn_Wf"].T).T,
        "b_gate": gate_rows(i["L0_xattn_bi"][:, None], i["L0_xattn_bf"][:, None]),
        "ln_scale": i["L0_xattn_ln_scale"][None],
        "w_expert": np.concatenate([flat(i["L0_ffn_select_weight"]), flat(i["L0_ffn_lora_update"]),
                                    i["L0_ffn_select_mean_diff"].T], 1),
        "debias": i["L0_ffn_debias_w"].T,
        "degen": np.concatenate([i["L0_ffn_lora_degen"].transpose(0, 2, 1).reshape(NX * NR, E),
                                 i["L0_ffn_bias_w"]]),
        "expert_rows": np.stack([i["L0_ffn_imp_center"], i["L0_ffn_imp_slope"],
                                 np.arange(NX, 0, -1, dtype=np.float32)]),
    }
    nc = bacc.Bacc("TRN2", target_bir_lowering=False, num_devices=1)
    args, ins = {}, {}
    for name, a in arrays.items():
        a = np.ascontiguousarray(a)
        ins[f"in_{name}"] = a
        args[name] = nc.dram_tensor(f"in_{name}", a.shape, mybir.dt.from_np(a.dtype), kind="ExternalInput").ap()
    out = nc.dram_tensor("out_dram", (NT, P, E), F32, kind="ExternalOutput").ap()
    bass_decoder(nc, out=out, **args)
    return run(nc, [ins], core_ids=[0]).results[0]["out_dram"]
```

```python
from collections import namedtuple
from contextlib import ExitStack

import concourse.bass as bass
from concourse import mybir

ALU = mybir.AluOpType
ACT = mybir.ActivationFunctionType
AX_X = mybir.AxisListType.X
F32 = mybir.dt.float32
F32R = mybir.dt.float32r
BF16 = mybir.dt.bfloat16

P = 128
NT = 64
E = 512
CH = E // P
H = 16
D = E // H
HD = D + 1
G = 16
GW = 32 + H
NX = 8
NR = 8
NW = 2 * NX * NR + NX
NL = NX * NR + NX
LN_EPS = 1e-5
ML_EPS = 1e-6

LAGS = 4
QK_BANKS = 4, 7, 6, 7
PADS = 7
PEEL = 6


class Tile:

    def __init__(self, k, regs=None, dma=None, u=None):
        self.k, self.regs, self.dma, self.u = k, regs, dma, u

    def older(self, n):
        return Tile(self.k - n, self.regs, self.dma, self.u)

    def parity(self):
        return self.k % 2

    def real(self):
        return self.regs is not None or 0 <= self.k < NT

    def index(self):
        return self.k if self.u is None else self.u * 2 + self.k


def upto(tile, back=0):
    if tile.regs is None:
        return min(max(tile.k + 1 - back, 0), NT)
    return tile.regs[tile.k + 1 - back]


def upto_quarter(tile, j):
    if tile.regs is None:
        return 4 * tile.k + j + 1
    return tile.regs[("quarter", 4 * tile.k + j + 1)]


def landed(tile, pieces):
    if tile.dma is None:
        return 16 * pieces * (tile.k // 2 + 1)
    return tile.dma[(pieces, tile.k // 2 + 1)]


def stored(tile):
    return 16 * tile.k if tile.dma is None else tile.dma[("out", tile.k)]


def bass_decoder(nc, x, ctx, wq, wk, wv, wo, bqkv, bo, rope, ident, mask_l, mask_r, head_rows,
                 w_gate, b_gate, ln_scale, w_expert, debias, degen, expert_rows, out):
    with ExitStack() as stack:
        def sb(name, shape, dt=F32):
            return stack.enter_context(nc.sbuf_tensor(name, shape, dt))

        def sem(name):
            return stack.enter_context(nc.semaphore(name))

        w_high = [sb(f"w{n}_high", [P, CH, E], F32R) for n in "qkvo"]
        w_low = [sb(f"w{n}_low", [P, CH, E], F32R) for n in "qkvo"]
        bias3 = sb("bias3", [P, 3 * E], BF16)
        bias_mid = sb("bias_mid", [1, 3 * E], BF16)
        ones_bf = sb("ones_bf", [P, P], BF16)
        ones_f = sb("ones_f", [P, P])
        bo_sb = sb("bo_sb", [P, E])
        rope_sb = sb("rope_sb", [P, 4, D])
        id_sb = sb("id_sb", [P, P])
        mask_l_sb = sb("mask_l_sb", [P, P], BF16)
        mask_r_sb = sb("mask_r_sb", [P, 4 * P], BF16)
        head_sb = sb("head_sb", [80, H, P], BF16)
        wg_sb = sb("wg_sb", [P, 3, CH, GW])
        wg_ctx = sb("wg_ctx", [P, CH, GW])
        bg_sb = sb("bg_sb", [GW, 1])
        lns_sb = sb("lns_sb", [P, E])
        wx_sb = sb("wx_sb", [P, CH, NW])
        debias_sb = sb("debias_sb", [P, CH, NX])
        wx_prod = sb("wx_prod", [P, CH, NW])
        wx_shift = sb("wx_shift", [P, NW])
        degen_sb = sb("degen_sb", [NL, E])
        xrow_sb = sb("xrow_sb", [P, 3, NX])
        half_neg = sb("half_neg", [P, H])
        zeros = sb("zeros", [H, P])

        xb = [sb(f"xb{i}", [P, E]) for i in range(2)]
        xr = [sb(f"xr{i}", [P, E]) for i in range(2)]
        xres = [sb(f"xres{i}", [P, E]) for i in range(2)]
        x_high = sb("x_high", [P, CH, P], F32R)
        x_low = sb("x_low", [P, CH, P], F32R)
        rot = [[sb(f"rot{n}{i}", [P, E]) for i in range(2)] for n in "qk"]
        QT = [sb(f"QT{i}", [P, CH, P]) for i in range(2)]
        KT = [sb(f"KT{i}", [P, CH, P]) for i in range(2)]
        VT = sb("VT", [P, CH, P])
        VG = [sb(f"VG{i}", [P, CH, P]) for i in range(2)]
        neg_max = sb("neg_max", [P, G])
        ex = sb("ex", [P, G, P])
        PT = sb("PT", [P, G, P])
        w_sum = sb("w_sum", [P, G])
        w_rec = sb("w_rec", [P, G])
        O_high = sb("O_high", [P, CH, P], F32R)
        O_low = sb("O_low", [P, CH, P], F32R)
        r1 = sb("r1", [P, E])
        st1 = sb("st1", [P, 6])
        mv1 = sb("mv1", [P, 2])
        ve1 = sb("ve1", [P, 1])
        rs1 = sb("rs1", [P, 1])
        x1 = [sb(f"x1_{i}", [P, E]) for i in range(2)]
        cb = [sb(f"cb{i}", [P, E]) for i in range(2)]
        c1 = [sb(f"c1_{i}", [P, H, HD]) for i in range(2)]
        x1T = sb("x1T", [P, CH, P])
        cT = sb("cT", [P, CH, P])
        gs = sb("gs", [GW, P])
        g_abs = sb("g_abs", [GW, P])
        g_exp = sb("g_exp", [GW, P])
        g_ln = sb("g_ln", [GW, P])
        log_f = sb("log_f", [H, P])
        Fs = sb("Fs", [H, P])
        a_row = sb("a_row", [H, P])
        M_row = sb("M_row", [H, P])
        FM = sb("FM", [H, P])
        m_rest = sb("m_rest", [32 + H, P])
        Mp = sb("Mp", [80, P], BF16)
        a_col = sb("a_col", [P, H])
        eFM = sb("eFM", [P, H])
        Dx = sb("Dx", [P, 4, CH, P])
        h_n0 = sb("h_n0", [P, H])
        h_n1 = sb("h_n1", [P, H])
        h_n2 = sb("h_n2", [P, H])
        h_rec = sb("h_rec", [P, H])
        hn = sb("hn", [P, H, D])
        h_sum = sb("h_sum", [P, H])
        cen = sb("cen", [P, H, D])
        cen2 = sb("cen2", [P, H, D])
        h_var = sb("h_var", [P, H])
        h_ve = sb("h_ve", [P, H])
        h_rs = sb("h_rs", [P, H])
        y2 = sb("y2", [P, E])
        r2 = sb("r2", [P, E])
        st2 = sb("st2", [P, 6])
        mv2 = sb("mv2", [P, 2])
        ve2 = sb("ve2", [P, 1])
        rs2 = sb("rs2", [P, 1])
        x2 = [sb(f"x2_{i}", [P, E]) for i in range(2)]
        rs2sq = sb("rs2sq", [P, 1])
        x2sq = [sb(f"x2sq{i}", [P, 1]) for i in range(2)]
        x2T = sb("x2T", [P, CH, P])
        fz = sb("fz", [P, 2 * NX * NR])
        fz2 = sb("fz2", [P, NX, NR])
        f_sc = sb("f_sc", [P, NX])
        f_n1 = sb("f_n1", [P, NX])
        f_n2 = sb("f_n2", [P, NX])
        f_n3 = sb("f_n3", [P, NX])
        f_s = sb("f_s", [P, NX])
        f_u = sb("f_u", [P, NX])
        f_v = sb("f_v", [P, NX])
        f_e = sb("f_e", [P, NX])
        f_e1 = sb("f_e1", [P, NX])
        gate = sb("gate", [P, NX])
        g_max = sb("g_max", [P, 1])
        g_key = sb("g_key", [P, NX])
        g_kmax = sb("g_kmax", [P, 1])
        g_rest = sb("g_rest", [P, 1])
        L = sb("L", [P, NL])
        LT = sb("LT", [NL, P])
        y3 = sb("y3", [P, E])
        st3 = sb("st3", [P, 6])
        mv3 = sb("mv3", [P, 2])
        ve3 = sb("ve3", [P, 1])
        rs3 = sb("rs3", [P, 1])
        yo = sb("yo", [P, E])

        bank = [stack.enter_context(nc.psum_tensor(f"bank{i}", [P, 512], F32)) for i in range(8)]

        once = """const_in w_in bias_step prod_set shift_ps
            shift_set pads_set high_set low_set""".split()
        each = """xT_ps xhigh_sb xlow_sb q_ps k_ps v_ps q_rot k_rot q_sum k_sum QT_sb KT_sb VT_sb VG_ps VG_sb xres_sb
            max_sb rec_sb O_ps Ohigh_sb Olow_sb proj_ps r1_sb st1_sb mv1_sb ve1_sb rs1_sb x1_sb
            x1T_ps x1T_sb cT_ps cT_sb c1_sb gate_ps gs_sb gabs_sb gexp_sb gln_sb logf_sb
            Fs_sb a_sb M_sb FM_sb Mhi_sb Mrest_sb Mmid2_sb Mp_sb aT_ps acol_sb eFM_sb
            hn0_sb hn1_sb hn2_sb hrec_sb hn_sb hsum_sb cen_sb cen2_sb hvar_sb hve_sb hrs_sb y1_sb y2_sb r2_sb
            st2_sb mv2_sb ve2_sb rs2_sb x2_sb rs2sq_sb
            x2T_ps x2T_sb F_ps fz_sb fz2_sb fn1_sb fn2_sb fn3_sb fs_sb fu_sb fv_sb fe_sb fe1_sb
            gate_sb gmax_sb gkey_sb gkmax_sb oh_sb L_sb LT_ps LT_sb Y_ps y3_sb st3_sb mv3_sb
            ve3_sb rs3_sb yo_sb""".split()
        four = "S_ps ex_sb exn_sb PT_ps PT_sb D_ps Dx_sb Dm_sb QK_ps C_sb".split()
        two = "H_ps x_in c_in r_in".split()
        semaphores = {n: sem(n) for n in once + each + ["y_out"]}
        semaphores |= {n: [sem(f"{n}{j}") for j in range(4)] for n in four}
        semaphores |= {n: [sem(f"{n}{j}") for j in range(2)] for n in two}
        s = namedtuple("Semaphores", semaphores)(**semaphores)

        w_in = [[ex[:, 4 * c:4 * c + 4, :].rearrange("p g n -> p (g n)") for c in range(CH)],
                [PT[:, 4 * c:4 * c + 4, :].rearrange("p g n -> p (g n)") for c in range(CH)],
                [Dx[:, c].rearrange("p c n -> p (c n)") for c in range(CH)],
                [y3[:], yo[:], r1[:], r2[:]]]
        bias_in = [t[0:1, :] for t in (rot[0][0], rot[0][1], rot[1][0])]
        bias_rest = [t[0:1, :] for t in (x1[0], x1[1], x2[0])]

        consts = [
            *[(bias_in[n], bqkv[:, n * E:(n + 1) * E]) for n in range(3)], (bo_sb[:], bo.broadcast_to([P, E])), (rope_sb[:], rope), (id_sb[:], ident),
            (mask_l_sb[:], mask_l), (mask_r_sb[:], mask_r), (head_sb[:], head_rows),
            (wg_sb[:], w_gate.rearrange("(m c p) n -> p m c n", p=P, c=CH)), (bg_sb[:], b_gate),
            (lns_sb[:], ln_scale.broadcast_to([P, E])), (wx_sb[:], w_expert.rearrange("(c p) n -> p c n", p=P)),
            (debias_sb[:], debias.rearrange("(c p) n -> p c n", p=P)), (degen_sb[:], degen),
            (xrow_sb[:], expert_rows.unsqueeze(0).broadcast_to([P, 3, NX])),
        ]
        CONST_IN = 16 * len(consts)

        def steps(eng, step, quarters=()):
            for t in range(PEEL):
                step(Tile(t))
            with eng.Fori(PEEL // 2, NT // 2) as u:
                regs = {k: eng.snap(u * 2 + k) for k in range(-LAGS - 1, 3)}
                regs |= {("quarter", k): eng.snap(u * 8 + k) for k in quarters}
                dma = {(n, k): eng.snap(u * (16 * n) + 16 * n * k) for n in (1, 4) for k in range(-1, 2)}
                dma |= {("out", k): eng.snap(u * 32 + 16 * k) for k in range(-LAGS, -LAGS + 2)}
                for k in range(2):
                    step(Tile(k, regs, dma, u))
            for t in range(NT, NT + LAGS):
                step(Tile(t))

        x_v = x.rearrange("b (s q) e -> b q s e", q=4)
        block = stack.enter_context(nc.Block())

        @block.sync
        def _(sp):
            for dst, src in consts:
                sp.dma_start(dst, src).then_inc(s.const_in, 16)

            def load_x(t):
                for q in range(4):
                    sp.dma_start(xb[t.parity()][32 * q:32 * q + 32, :], x_v[t.index(), q]).then_inc(
                        s.x_in[t.parity()], 16)

            def load_res(t):
                sp.dma_start(xr[t.parity()][:], x[t.index()]).then_inc(s.r_in[t.parity()], 16)

            def load_ctx(t):
                sp.dma_start(cb[t.parity()][:], ctx[t.index()]).then_inc(s.c_in[t.parity()], 16)

            def store(t):
                sp.wait_ge(s.yo_sb, upto(t))
                sp.dma_start(out[t.index()], yo[:]).then_inc(s.y_out, 16)

            load_x(Tile(0))
            load_res(Tile(0))
            for n, w in enumerate((wq, wk, wv, wo)):
                for c in range(CH):
                    sp.dma_start(w_in[n][c], w[c * P:(c + 1) * P]).then_inc(s.w_in, 16)

            def step(a):
                nxt, c, f = a.older(-1), a.older(1), a.older(4)
                if nxt.real() and not (nxt.regs is None and nxt.k >= NT):
                    sp.wait_ge(s.xT_ps, upto(nxt, 2))
                    load_x(nxt)
                    sp.wait_ge(s.xres_sb, upto(nxt, 2))
                    load_res(nxt)
                if c.real():
                    sp.wait_ge(s.cT_ps, upto(c, 2))
                    sp.wait_ge(s.c1_sb, upto(c, 2))
                    load_ctx(c)
                if f.real():
                    store(f)

            for t in range(PEEL):
                step(Tile(t))
            with sp.Fori(PEEL // 2, NT // 2 - 1) as u:
                regs = {k: sp.snap(u * 2 + k) for k in range(-LAGS - 1, 3)}
                for k in range(2):
                    step(Tile(k, regs, None, u))
            for t in range(NT - 2, NT + LAGS):
                step(Tile(t))
            sp.wait_ge(s.y_out, 16 * NT)

        @block.tensor
        def _(pe):
            mm = nc.tensor.matmul

            def transposes(dst, src):
                for c in range(CH):
                    last = nc.tensor.transpose(dst[:, c * P:(c + 1) * P], src[:, c * P:(c + 1) * P], id_sb[:])
                return last

            def p_xT(a):
                pe.wait_ge(s.x_in[a.parity()], landed(a, 4))
                pe.wait_ge(s.C_sb[0], upto(a, 3))
                transposes(bank[4], xb[a.parity()]).then_inc(s.xT_ps, 1)

            def p_bias(n, b):
                mm(bank[b][:], ones_bf[:], bias3[:, n * E:(n + 1) * E], start=True, stop=False)

            def high_pass(b, x_t, n, c, first=False):
                stationary = x_t[:, c, :]
                mm(bank[b][:], stationary, w_high[n][:, c, :], start=first, stop=False)
                mm(bank[b][:], stationary, w_low[n][:, c, :], start=False, stop=False)

            def low_passes(b, x_low_t, n):
                for c in range(CH):
                    last = mm(bank[b][:], x_low_t[:, c, :], w_high[n][:, c, :], start=False,
                              stop=(c == CH - 1))
                return last

            def p_proj(a, n, b, out_sem):
                p_bias(n, b)
                for c in range(CH):
                    high_pass(b, x_high, n, c)
                low_passes(b, x_low, n).then_inc(out_sem, 1)

            def p_q_r_H(a, e):
                if a.k == 0 and a.regs is None:
                    pe.wait_ge(s.low_set, 4)
                if a.real():
                    pe.wait_ge(s.xhigh_sb, upto(a))
                    pe.wait_ge(s.cT_sb, upto(a, 2))
                    p_bias(0, 6)
                if e.real():
                    for j in range(4):
                        pe.wait_ge(s.C_sb[j], upto(e))
                    pe.wait_ge(s.c1_sb, upto(e))
                for c in range(CH):
                    if a.real():
                        high_pass(6, x_high, 0, c)
                    if e.real():
                        for h in range(4 * c, 4 * c + 4):
                            m = h // 8
                            if h == 8:
                                pe.wait_ge(s.xlow_sb, upto(e, -3))
                            last_h = mm(bank[(7, 4)[m]][:, (h % 8) * HD:(h % 8 + 1) * HD], Dx[:, h % 4, h // 4, :],
                                        c1[e.parity()][:, h, :], start=True, stop=True)
                            if h % 8 == 7:
                                last_h.then_inc(s.H_ps[m], 1)
                if a.real():
                    pe.wait_ge(s.xlow_sb, upto(a))
                    low_passes(6, x_low, 0).then_inc(s.q_ps, 1)

            def p_k(a):
                pe.wait_ge(s.hn_sb, upto(a, 3))
                p_proj(a, 1, 4, s.k_ps)

            def p_v(a):
                pe.wait_ge(s.q_rot, upto(a))
                p_proj(a, 2, 6, s.v_ps)

            def p_VG(a):
                pe.wait_ge(s.VT_sb, upto(a))
                pe.wait_ge(s.k_rot, upto(a))
                for c in range(CH):
                    last = nc.tensor.transpose(bank[4][:, c * P:(c + 1) * P],
                                               VT[:, c, :], id_sb[:])
                last.then_inc(s.VG_ps, 1)

            def a_S(b, parts):
                pe.wait_ge(s.QT_sb, upto(b))
                pe.wait_ge(s.KT_sb, upto(b))
                q_v, k_v = QT[b.parity()], KT[b.parity()]
                for j in parts:
                    pe.wait_ge(s.Dx_sb[j], upto(b, 2))
                    mm(bank[j][:], mask_l_sb[:], mask_r_sb[:], start=True, stop=True, skip_group_check=True)
                    rows = slice(32 * j, 32 * j + 32)
                    for c in range(CH):
                        last = mm(bank[j][:, c * P:(c + 1) * P], q_v[rows, c, :], k_v[rows, c, :],
                                  start=False, stop=True, skip_group_check=True)
                    last.then_inc(s.S_ps[j], 1)

            def a_PT(b):
                for j in range(4):
                    pe.wait_ge(s.exn_sb[j], upto(b))
                    for c in range(CH):
                        last = nc.tensor.transpose(bank[j][:, c * P:(c + 1) * P], ex[:, 4 * j + c, :], id_sb[:])
                    last.then_inc(s.PT_ps[j], 1)

            def a_O(b):
                pe.wait_ge(s.VG_sb, upto(b))
                pe.wait_ge(s.VT_sb, upto(b, -1))
                for j in range(4):
                    pe.wait_ge(s.PT_sb[j], upto(b))
                    for c in range(CH):
                        last = mm(bank[6][32 * j:32 * j + 32, c * P:(c + 1) * P],
                                  VG[b.parity()][:, c, 32 * j:32 * j + 32], PT[:, 4 * j + c, :],
                                  start=True, stop=True, tile_position=(0, 32 * j))
                last.then_inc(s.O_ps, 1)

            def a_proj_m_QK(b, c):
                if b.real():
                    pe.wait_ge(s.Ohigh_sb, upto(b))
                    pe.wait_ge(s.LT_sb, upto(b, 3))
                    if b.regs is None:
                        pe.wait_ge(s.acol_sb, upto(b, 1))
                        pe.wait_ge(s.eFM_sb, upto(b, 1))
                for n in range(CH):
                    if b.real():
                        high_pass(5, O_high, 3, n, first=(n == 0))
                    if c.real() and n < 3:
                        m_QK(c, n + 1)
                if b.real():
                    pe.wait_ge(s.Olow_sb, upto(b))
                    low_passes(5, O_low, 3).then_inc(s.proj_ps, 1)

            def m_cT(c):
                pe.wait_ge(s.c_in[c.parity()], landed(c, 1))
                pe.wait_ge(s.C_sb[2], upto(c, 1))
                transposes(bank[6], cb[c.parity()]).then_inc(s.cT_ps, 1)

            def m_x1T(c):
                pe.wait_ge(s.x1_sb, upto(c))
                pe.wait_ge(s.r1_sb, upto(c))
                transposes(bank[5], x1[c.parity()]).then_inc(s.x1T_ps, 1)

            def m_gate(c):
                pe.wait_ge(s.x1T_sb, upto(c))
                pe.wait_ge(s.cT_sb, upto(c))
                for n in range(CH):
                    mm(bank[5][0:GW, 0:P], wg_sb[:, 0, n, :], x1T[:, n, :], start=(n == 0), stop=False)
                for n in range(CH):
                    last = mm(bank[5][0:GW, 0:P], wg_ctx[:, n, :], cT[:, n, :], start=False, stop=(n == CH - 1))
                last.then_inc(s.gate_ps, 1)

            def m_aT(c):
                pe.wait_ge(s.pads_set, PADS)
                pe.wait_ge(s.FM_sb, upto(c))
                nc.tensor.transpose(bank[5][:, 0:H], a_row[:], id_sb[0:H, 0:H])
                nc.tensor.transpose(bank[5][:, H:2 * H], FM[:], id_sb[0:H, 0:H]).then_inc(s.aT_ps, 1)

            def m_D(c):
                pe.wait_ge(s.Mp_sb, upto(c))
                pe.wait_ge(s.Mmid2_sb, upto(c))
                for j in range(4):
                    pe.wait_ge(s.PT_sb[j], upto(c, -1))
                    for n in range(CH):
                        last = mm(bank[j][:, n * P:(n + 1) * P], head_sb[:, 4 * n + j, :], Mp[:],
                                  start=True, stop=True)
                    last.then_inc(s.D_ps[j], 1)

            def m_QK(c, j):
                free = ((s.VG_sb, upto(c, -2)), (s.fn1_sb, upto(c, 2)), (s.y3_sb, upto(c, 2)), (s.C_sb[1], upto(c)))
                pe.wait_ge(*free[j])
                if j == 1 and c.regs is None:
                    pe.wait_ge(s.hn_sb, upto(c, 1))
                if j == 2 and c.regs is None:
                    pe.wait_ge(s.Olow_sb, upto(c, -1))
                rows = slice(32 * j, 32 * j + 32)
                b = QK_BANKS[j]
                for n in range(CH):
                    last = mm(bank[b][:, n * P:(n + 1) * P], cT[rows, n, :], x1T[rows, n, :], start=True, stop=True)
                last.then_inc(s.QK_ps[j], 1)

            def x_x2T(f):
                pe.wait_ge(s.x2_sb, upto(f))
                pe.wait_ge(s.hn_sb, upto(f, -1))
                transposes(bank[7], x2[f.parity()]).then_inc(s.x2T_ps, 1)

            def x_F(f):
                pe.wait_ge(s.x2T_sb, upto(f))
                for c in range(CH):
                    last = mm(bank[7][:, 0:NW], x2T[:, c, :], wx_sb[:, c, :], start=(c == 0), stop=(c == CH - 1))
                last.then_inc(s.F_ps, 1)

            def x_LT(f):
                pe.wait_ge(s.L_sb, upto(f))
                pe.wait_ge(s.oh_sb, upto(f))
                pe.wait_ge(s.acol_sb, upto(f, -2))
                pe.wait_ge(s.eFM_sb, upto(f, -2))
                nc.tensor.transpose(bank[5][0:NL, 0:P], L[:], id_sb[:]).then_inc(s.LT_ps, 1)

            def x_Y(f):
                pe.wait_ge(s.LT_sb, upto(f))
                pe.wait_ge(s.Olow_sb, upto(f, -3))
                mm(bank[6][:], LT[:], degen_sb[:], start=True, stop=True).then_inc(s.Y_ps, 1)

            def settle(a):
                pe.wait_ge(s.VG_sb, upto(a, 1))
                pe.wait_ge(s.Olow_sb, upto(a, 2))
                pe.wait_ge(s.fn1_sb, upto(a, 5))
                pe.wait_ge(s.y3_sb, upto(a, 5))
                if a.k >= NT:
                    for j in range(4):
                        pe.wait_ge(s.Dx_sb[j], upto(a, 3))
                        pe.wait_ge(s.C_sb[j], upto(a, 3))

            pe.wait_ge(s.const_in, CONST_IN)
            pe.wait_ge(s.prod_set, 3)
            pe.wait_ge(s.pads_set, PADS)
            for c in range(CH):
                last = mm(bank[0][:, 0:NW], ones_f[:], wx_prod[:, c, :], start=(c == 0), stop=(c == CH - 1))
            last.then_inc(s.shift_ps, 1)
            pe.wait_ge(s.shift_set, 1)
            pe.wait_ge(s.bias_step, 15)

            def step(a):
                b, c, e, f = a.older(1), a.older(2), a.older(3), a.older(4)
                if a.regs is None:
                    settle(a)
                if a.real():
                    p_xT(a)
                if b.real():
                    a_S(b, (0, 1))
                if c.real():
                    m_cT(c)
                if b.real():
                    a_S(b, (2, 3))
                if c.real():
                    m_x1T(c)
                p_q_r_H(a, e)
                if c.real():
                    m_gate(c)
                if f.real():
                    x_x2T(f)
                if a.real():
                    p_k(a)
                if f.real():
                    x_F(f)
                if a.real():
                    p_v(a)
                if b.real():
                    a_PT(b)
                if c.real():
                    m_aT(c)
                if a.real():
                    p_VG(a)
                if b.real():
                    a_O(b)
                if c.real():
                    m_D(c)
                if f.real():
                    x_LT(f)
                if c.real():
                    m_QK(c, 0)
                if f.real():
                    x_Y(f)
                a_proj_m_QK(b, c)

            steps(pe, step)

        @block.scalar
        def _(act):
            def copy4(dst, b):
                return nc.scalar.activation(dst, bank[b][:], ACT.Copy)

            def p_xT(a):
                act.wait_ge(s.xT_ps, upto(a))
                act.wait_ge(s.v_ps, upto(a, 1))
                copy4(x_high[:].rearrange("p c n -> p (c n)"), 4).then_inc(s.xhigh_sb, 1)

            def p_VG(a):
                act.wait_ge(s.VG_ps, upto(a))
                act.wait_ge(s.O_ps, upto(a, 2))
                copy4(VG[a.parity()][:].rearrange("p c n -> p (c n)"), 4).then_inc(s.VG_sb, 1)

            def a_exp(b, j):
                act.wait_ge(s.max_sb, upto_quarter(b, j))
                act.wait_ge(s.PT_ps[j], upto(b, 1))
                for c in range(CH):
                    g = 4 * j + c
                    last = nc.scalar.activation(ex[:, g, :], bank[j][:, c * P:(c + 1) * P], ACT.Exp,
                                                bias=neg_max[:, g:g + 1], accum_out=w_sum[:, g:g + 1])
                last.then_inc(s.ex_sb[j], 1)

            def a_PT(b, j):
                act.wait_ge(s.PT_ps[j], upto(b))
                act.wait_ge(s.O_ps, upto(b, 1))
                copy4(PT[:, 4 * j:4 * j + 4, :].rearrange("p g m -> p (g m)"), j).then_inc(s.PT_sb[j], 1)

            def a_OT(b):
                act.wait_ge(s.O_ps, upto(b))
                act.wait_ge(s.proj_ps, upto(b, 1))
                copy4(O_high[:].rearrange("p c n -> p (c n)"), 6).then_inc(s.Ohigh_sb, 1)

            def m_x1T(c):
                act.wait_ge(s.x1T_ps, upto(c))
                act.wait_ge(s.QK_ps[3], upto(c, 1))
                copy4(x1T[:].rearrange("p c n -> p (c n)"), 5).then_inc(s.x1T_sb, 1)

            def m_cT(c):
                act.wait_ge(s.cT_ps, upto(c))
                act.wait_ge(s.QK_ps[3], upto(c, 1))
                copy4(cT[:].rearrange("p c n -> p (c n)"), 6).then_inc(s.cT_sb, 1)

            def m_gate(c):
                act.wait_ge(s.gabs_sb, upto(c))
                nc.scalar.activation(g_exp[32:GW, :], g_abs[32:GW, :], ACT.Exp).then_inc(s.gexp_sb, 1)
                act.wait_ge(s.gexp_sb, upto(c))
                nc.scalar.activation(g_ln[32:GW, :], g_exp[32:GW, :], ACT.Ln, bias=1.0).then_inc(s.gln_sb, 1)

            def m_eFM(c):
                act.wait_ge(s.acol_sb, upto(c))
                act.wait_ge(s.hn1_sb, upto(c, 1))
                nc.scalar.activation(eFM[:], bank[5][:, H:2 * H], ACT.Exp, scale=-1.0).then_inc(s.eFM_sb, 1)

            def m_Dx(c, j):
                act.wait_ge(s.D_ps[j], upto(c))
                act.wait_ge(s.acol_sb, upto(c))
                act.wait_ge(s.H_ps[1], upto(c, 1))
                for n in range(CH):
                    h = 4 * n + j
                    last = nc.scalar.activation(Dx[:, j, n, :], bank[j][:, n * P:(n + 1) * P], ACT.Exp,
                                                bias=a_col[:, h:h + 1])
                last.then_inc(s.Dx_sb[j], 1)

            def r_sq(e):
                act.wait_ge(s.cen_sb, upto(e))
                act.wait_ge(s.hvar_sb, upto(e, 1))
                nc.scalar.activation(cen2[:], cen[:], ACT.Square).then_inc(s.cen2_sb, 1)

            def x_x2T(f):
                act.wait_ge(s.x2T_ps, upto(f))
                act.wait_ge(s.F_ps, upto(f, 1))
                copy4(x2T[:].rearrange("p c n -> p (c n)"), 7).then_inc(s.x2T_sb, 1)

            def x_exp(f):
                act.wait_ge(s.fv_sb, upto(f))
                act.wait_ge(s.fe1_sb, upto(f, 1))
                nc.scalar.activation(f_e[:], f_v[:], ACT.Exp, scale=-1.0).then_inc(s.fe_sb, 1)

            nc.scalar.preload_act_table_set("natural_log_exp_and_others")
            act.wait_ge(s.const_in, CONST_IN)
            act.wait_ge(s.w_in, 16 * 4 * CH)
            for n in range(4):
                for c in range(CH):
                    last = nc.scalar.activation(w_high[n][:, c, :], w_in[n][c], ACT.Copy)
                last.then_inc(s.high_set, 1)

            def step(a):
                b, c, e, f = a.older(1), a.older(2), a.older(3), a.older(4)
                if a.real():
                    p_xT(a)
                if c.real():
                    m_cT(c)
                if b.real():
                    a_exp(b, 0)
                    a_exp(b, 1)
                if c.real():
                    m_x1T(c)
                if b.real():
                    a_exp(b, 2)
                    a_exp(b, 3)
                if f.real():
                    x_x2T(f)
                if c.real():
                    m_gate(c)
                if e.real():
                    r_sq(e)
                if b.real():
                    a_PT(b, 0)
                    a_PT(b, 1)
                if f.real():
                    x_exp(f)
                if b.real():
                    a_PT(b, 2)
                    a_PT(b, 3)
                if a.real():
                    p_VG(a)
                if c.real():
                    m_eFM(c)
                if b.real():
                    a_OT(b)
                if c.real():
                    for j in range(4):
                        m_Dx(c, j)

            steps(act, step, range(-3, 5))

        @block.gpsimd
        def _(pool):
            tt = nc.gpsimd.tensor_tensor

            def p_xres(a):
                pool.wait_ge(s.r_in[a.parity()], landed(a, 1))
                pool.wait_ge(s.r1_sb, upto(a, 2))
                tt(xres[a.parity()][:], xr[a.parity()][:], bo_sb[:], ALU.add).then_inc(s.xres_sb, 1)

            def p_rot(a, n):
                pool.wait_ge((s.q_rot, s.k_rot)[n], upto(a))
                pool.wait_ge((s.QT_sb, s.KT_sb)[n], upto(a, 1))
                tt(rot[n][0][:], rot[n][0][:], rot[n][1][:], ALU.add).then_inc((s.q_sum, s.k_sum)[n], 1)

            def m_c1(c):
                pool.wait_ge(s.c_in[c.parity()], landed(c, 1))
                pool.wait_ge(s.H_ps[1], upto(c, 2))
                tt(c1[c.parity()][:, :, 0:D], cb[c.parity()][:].rearrange("p (h d) -> p h d", d=D),
                   ones_f[:, 0:1].unsqueeze(2).broadcast_to([P, H, D]), ALU.mult).then_inc(s.c1_sb, 1)

            def a_scale(b, j):
                pool.wait_ge(s.rec_sb, upto_quarter(b, j))
                tt(ex[:, 4 * j:4 * j + 4, :], ex[:, 4 * j:4 * j + 4, :],
                   w_rec[:, 4 * j:4 * j + 4].unsqueeze(2).broadcast_to([P, 4, P]), ALU.mult).then_inc(s.exn_sb[j], 1)

            def m_mask(c, j):
                pool.wait_ge(s.pads_set, PADS)
                pool.wait_ge(s.Dx_sb[j], upto(c))
                nc.gpsimd.affine_select(Dx[:, j], Dx[:, j], compare_op=ALU.is_ge, fill=0.0, base=0,
                                        pattern=[[0, CH], [1, P]],
                                        channel_multiplier=-1).then_inc(s.Dm_sb[j], 1)

            def r_head(e):
                pool.wait_ge(s.hve_sb, upto(e))
                pool.wait_ge(s.y1_sb, upto(e, 1))
                tt(h_rs[:], h_ve[:], half_neg[:], ALU.pow).then_inc(s.hrs_sb, 1)
                pool.wait_ge(s.hrs_sb, upto(e))
                pool.wait_ge(s.cen_sb, upto(e))
                tt(cen[:], cen[:], h_rs[:].unsqueeze(2).broadcast_to([P, H, D]), ALU.mult).then_inc(s.y1_sb, 1)
                pool.wait_ge(s.y1_sb, upto(e))
                pool.wait_ge(s.r2_sb, upto(e, 1))
                tt(y2[:], cen[:].rearrange("p h d -> p (h d)"), lns_sb[:], ALU.mult).then_inc(s.y2_sb, 1)
                pool.wait_ge(s.y2_sb, upto(e))
                pool.wait_ge(s.x1_sb, upto(e))
                pool.wait_ge(s.x2_sb, upto(e, 1))
                tt(r2[:], y2[:], x1[e.parity()][:], ALU.add).then_inc(s.r2_sb, 1)

            def rsqrt(t, ve, rs, ve_sem, rs_sem, used):
                pool.wait_ge(ve_sem, upto(t))
                pool.wait_ge(used, upto(t, 1))
                tt(rs[:], ve[:], half_neg[:, 0:1], ALU.pow).then_inc(rs_sem, 1)

            pool.wait_ge(s.const_in, CONST_IN)
            nc.gpsimd.memset(half_neg[:], -0.5).then_inc(s.pads_set, 1)
            for i in range(2):
                last = nc.gpsimd.memset(c1[i][:], 1.0)
            last.then_inc(s.pads_set, 1)
            tt(wg_ctx[:], wg_sb[:, 1], wg_sb[:, 2], ALU.add).then_inc(s.pads_set, 1)
            pool.wait_ge(s.pads_set, PADS)
            pool.wait_ge(s.high_set, 4)
            for c in range(CH):
                last = tt(w_low[3][:, c, :], w_in[3][c], w_high[3][:, c, :], ALU.subtract)
            last.then_inc(s.low_set, 1)

            def step(a):
                b, c, e, f = a.older(1), a.older(2), a.older(3), a.older(4)
                if a.real():
                    p_xres(a)
                if c.real():
                    m_c1(c)
                if b.real():
                    for j in range(4):
                        a_scale(b, j)
                if a.real():
                    p_rot(a, 0)
                if e.real():
                    r_head(e)
                if a.real():
                    p_rot(a, 1)
                if c.real():
                    for j in range(4):
                        m_mask(c, j)
                if f.real():
                    rsqrt(f, ve3, rs3, s.ve3_sb, s.rs3_sb, s.yo_sb)
                if e.real():
                    rsqrt(e, ve2, rs2, s.ve2_sb, s.rs2_sb, s.x2_sb)
                if b.real():
                    rsqrt(b, ve1, rs1, s.ve1_sb, s.rs1_sb, s.x1_sb)

            steps(pool, step, range(-3, 5))

        @block.vector
        def _(dve):
            tt = nc.vector.tensor_tensor
            ts = nc.vector.tensor_scalar
            stt = nc.vector.scalar_tensor_tensor
            red = nc.vector.tensor_reduce

            def rotate(t, n, b, ps, done, summed, part):
                src = bank[b][:].rearrange("p (h d) -> p h d", d=D)
                cos = rope_sb[:, 2 * n, :].unsqueeze(1).broadcast_to([P, H, D])
                sin = rope_sb[:, 2 * n + 1, :].unsqueeze(1).broadcast_to([P, H, D])
                other = rot[n][1][:].rearrange("p (h d) -> p h d", d=D)
                if part == 0:
                    dve.wait_ge(ps, upto(t))
                    dve.wait_ge(summed, upto(t, 1))
                    tt(rot[n][0][:].rearrange("p (h d) -> p h d", d=D), src, cos, ALU.mult)
                if part == 1:
                    tt(other[:, :, 0:D // 2], src[:, :, D // 2:D], sin[:, :, 0:D // 2], ALU.mult)
                if part == 2:
                    tt(other[:, :, D // 2:D], src[:, :, 0:D // 2], sin[:, :, D // 2:D], ALU.mult).then_inc(done, 1)

            def p_q(a):
                for part in range(3):
                    rotate(a, 0, 6, s.q_ps, s.q_rot, s.q_sum, part)

            def p_k(a, part):
                rotate(a, 1, 4, s.k_ps, s.k_rot, s.k_sum, part)

            def by_group(t):
                return t[:].rearrange("p c (h i) -> p h i c", i=8)

            def p_T(a, n):
                dve.wait_ge((s.q_sum, s.k_sum)[n], upto(a))
                dve.wait_ge(s.S_ps[3], upto(a, 2))
                nc.vector.transpose(by_group((QT, KT)[n][a.parity()]), rot[n][0][:]).then_inc((s.QT_sb, s.KT_sb)[n], 1)

            def p_VT(a):
                dve.wait_ge(s.v_ps, upto(a))
                dve.wait_ge(s.VG_ps, upto(a, 1))
                nc.vector.transpose(by_group(VT), bank[6][:]).then_inc(s.VT_sb, 1)

            def low_part(t, b, high, low, high_sem, low_sem, used):
                dve.wait_ge(high_sem, upto(t))
                dve.wait_ge(used, upto(t, 1))
                tt(low[:].rearrange("p c n -> p (c n)"), bank[b][:], high[:].rearrange("p c n -> p (c n)"),
                   ALU.subtract).then_inc(low_sem, 1)

            def p_low(a):
                low_part(a, 4, x_high, x_low, s.xhigh_sb, s.xlow_sb, s.v_ps)

            def a_low(b):
                low_part(b, 6, O_high, O_low, s.Ohigh_sb, s.Olow_sb, s.proj_ps)

            def a_max(b, j):
                dve.wait_ge(s.S_ps[j], upto(b))
                dve.wait_ge(s.ex_sb[j], upto(b, 1))
                red(neg_max[:, 4 * j:4 * j + 4], bank[j][:].rearrange("p (g n) -> p g n", n=P), AX_X, ALU.max,
                    negate=True).then_inc(s.max_sb, 1)

            def a_rec(b, j):
                dve.wait_ge(s.ex_sb[j], upto(b))
                nc.vector.reciprocal(w_rec[:, 4 * j:4 * j + 4], w_sum[:, 4 * j:4 * j + 4]).then_inc(s.rec_sb, 1)

            def norm_stats(t, r, st, mv, ve, st_sem, mv_sem, ve_sem):
                nc.vector.bn_stats(st[:], r[:]).then_inc(st_sem, 1)
                dve.wait_ge(s.pads_set, PADS)
                dve.wait_ge(st_sem, upto(t))
                nc.vector.bn_aggr(mv[:], st[:]).then_inc(mv_sem, 1)
                dve.wait_ge(mv_sem, upto(t))
                ts(ve[:], mv[:, 1:2], LN_EPS, None, ALU.add).then_inc(ve_sem, 1)

            def a_r1(b):
                dve.wait_ge(s.proj_ps, upto(b))
                dve.wait_ge(s.xres_sb, upto(b))
                tt(r1[:], bank[5][:], xres[b.parity()][:], ALU.add).then_inc(s.r1_sb, 1)
                dve.wait_ge(s.r1_sb, upto(b))
                norm_stats(b, r1, st1, mv1, ve1, s.st1_sb, s.mv1_sb, s.ve1_sb)

            def a_x1(b):
                dve.wait_ge(s.rs1_sb, upto(b))
                dve.wait_ge(s.r2_sb, upto(b, 2))
                ts(x1[b.parity()][:], r1[:], mv1[:, 0:1], rs1[:], ALU.subtract, ALU.mult).then_inc(s.x1_sb, 1)

            def m_gs(c):
                dve.wait_ge(s.gate_ps, upto(c))
                ts(gs[:], bank[5][0:GW, 0:P], bg_sb[:], None, ALU.add).then_inc(s.gs_sb, 1)
                dve.wait_ge(s.gs_sb, upto(c))
                stt(out=g_abs[32:GW, :], in0=gs[32:GW, :], scalar=-1.0, in1=gs[32:GW, :], op0=ALU.mult,
                    op1=ALU.min).then_inc(s.gabs_sb, 1)

            def m_logf(c):
                dve.wait_ge(s.gln_sb, upto(c))
                stt(out=log_f[:], in0=gs[32:GW, :], scalar=0.0, in1=g_ln[32:GW, :], op0=ALU.min,
                    op1=ALU.subtract).then_inc(s.logf_sb, 1)

            def m_scan(c, e):
                dve.wait_ge(s.logf_sb, upto(c))
                dve.wait_ge(s.aT_ps, upto(c, 1))
                dve.wait_ge(s.pads_set, PADS)
                nc.vector.tensor_tensor_scan(Fs[:], log_f[:], zeros[:], 0.0, ALU.add,
                                             ALU.add).then_inc(s.Fs_sb, 1)
                if e.real():
                    r_var(e)
                dve.wait_ge(s.Fs_sb, upto(c))
                tt(a_row[:], gs[0:H, :], Fs[:], ALU.subtract).then_inc(s.a_sb, 1)
                dve.wait_ge(s.a_sb, upto(c))
                nc.vector.tensor_tensor_scan(M_row[:], a_row[:], a_row[:], -3.0e38, ALU.max,
                                             ALU.max).then_inc(s.M_sb, 1)
                dve.wait_ge(s.M_sb, upto(c))
                tt(FM[:], Fs[:], M_row[:], ALU.add).then_inc(s.FM_sb, 1)

            def m_parts(c, a):
                dve.wait_ge(s.D_ps[3], upto(c, 1))
                ts(Mp[0:H, :], M_row[:], -1.0, None, ALU.mult).then_inc(s.Mhi_sb, 1)
                if a.real():
                    p_k(a, 0)
                dve.wait_ge(s.Mhi_sb, upto(c))
                stt(out=m_rest[32:32 + H, :], in0=M_row[:], scalar=-1.0, in1=Mp[0:H, :], op0=ALU.mult,
                    op1=ALU.subtract).then_inc(s.Mrest_sb, 1)
                if a.real():
                    p_k(a, 1)
                dve.wait_ge(s.Mrest_sb, upto(c))
                nc.vector.tensor_copy(Mp[32:32 + H, :], m_rest[32:32 + H, :]).then_inc(s.Mmid2_sb, 1)
                if a.real():
                    p_k(a, 2)
                dve.wait_ge(s.Mmid2_sb, upto(c))
                tt(Mp[64:64 + H, :], m_rest[32:32 + H, :], Mp[32:32 + H, :], ALU.subtract).then_inc(s.Mp_sb, 1)

            def m_acol(c):
                dve.wait_ge(s.aT_ps, upto(c))
                dve.wait_ge(s.Dx_sb[3], upto(c, 1))
                nc.vector.tensor_copy(a_col[:], bank[5][:, 0:H]).then_inc(s.acol_sb, 1)

            def m_C(c, j):
                dve.wait_ge(s.QK_ps[j], upto(c))
                dve.wait_ge(s.Dm_sb[j], upto(c))
                stt(out=Dx[:, j], in0=bank[QK_BANKS[j]][:].rearrange("p (c n) -> p c n", n=P),
                    scalar=float(D) ** -0.5, in1=Dx[:, j], op0=ALU.mult, op1=ALU.mult).then_inc(s.C_sb[j], 1)

            def r_h(e):
                dve.wait_ge(s.eFM_sb, upto(e))
                for m in range(2):
                    dve.wait_ge(s.H_ps[m], upto(e))
                    hs = bank[(7, 4)[m]][:, 0:8 * HD].rearrange("p (h d) -> p h d", d=HD)
                    last = stt(out=h_n0[:, 8 * m:8 * m + 8], in0=hs[:, :, D], scalar=-1.0,
                               in1=eFM[:, 8 * m:8 * m + 8], op0=ALU.mult, op1=ALU.max)
                last.then_inc(s.hn0_sb, 1)
                dve.wait_ge(s.hn0_sb, upto(e))
                for m in range(2):
                    hs = bank[(7, 4)[m]][:, 0:8 * HD].rearrange("p (h d) -> p h d", d=HD)
                    last = tt(h_n1[:, 8 * m:8 * m + 8], hs[:, :, D], h_n0[:, 8 * m:8 * m + 8], ALU.max)
                last.then_inc(s.hn1_sb, 1)
                dve.wait_ge(s.hn1_sb, upto(e))
                ts(h_n2[:], h_n1[:], ML_EPS, None, ALU.add).then_inc(s.hn2_sb, 1)
                dve.wait_ge(s.hn2_sb, upto(e))
                nc.vector.reciprocal(h_rec[:], h_n2[:]).then_inc(s.hrec_sb, 1)
                dve.wait_ge(s.hrec_sb, upto(e))
                for m in range(2):
                    hs = bank[(7, 4)[m]][:, 0:8 * HD].rearrange("p (h d) -> p h d", d=HD)
                    last = tt(hn[:, 8 * m:8 * m + 8, :], hs[:, :, 0:D],
                              h_rec[:, 8 * m:8 * m + 8].unsqueeze(2).broadcast_to([P, 8, D]), ALU.mult)
                last.then_inc(s.hn_sb, 1)
                dve.wait_ge(s.hn_sb, upto(e))
                red(h_sum[:], hn[:], AX_X, ALU.add).then_inc(s.hsum_sb, 1)
                dve.wait_ge(s.hsum_sb, upto(e))
                dve.wait_ge(s.y2_sb, upto(e, 1))
                stt(out=cen[:], in0=h_sum[:].unsqueeze(2).broadcast_to([P, H, D]), scalar=-1.0 / D, in1=hn[:],
                    op0=ALU.mult, op1=ALU.add).then_inc(s.cen_sb, 1)

            def r_var(e):
                dve.wait_ge(s.cen2_sb, upto(e))
                red(h_var[:], cen2[:], AX_X, ALU.add).then_inc(s.hvar_sb, 1)
                dve.wait_ge(s.hvar_sb, upto(e))
                dve.wait_ge(s.hrs_sb, upto(e, 1))
                ts(h_ve[:], h_var[:], 1.0 / D, ML_EPS, ALU.mult, ALU.add).then_inc(s.hve_sb, 1)

            def r_r2(e):
                dve.wait_ge(s.r2_sb, upto(e))
                norm_stats(e, r2, st2, mv2, ve2, s.st2_sb, s.mv2_sb, s.ve2_sb)

            def r_x2(e):
                dve.wait_ge(s.rs2_sb, upto(e))
                tt(rs2sq[:], rs2[:], rs2[:], ALU.mult).then_inc(s.rs2sq_sb, 1)
                dve.wait_ge(s.rs2sq_sb, upto(e))
                ts(x2sq[e.parity()][:], mv2[:, 1:2], rs2sq[:], float(E), ALU.mult, ALU.mult)
                dve.wait_ge(s.x2T_ps, upto(e, 2))
                ts(x2[e.parity()][:], r2[:], mv2[:, 0:1], rs2[:], ALU.subtract, ALU.mult).then_inc(s.x2_sb, 1)

            def x_choose(f):
                dve.wait_ge(s.F_ps, upto(f))
                nw = NX * NR
                tt(fz[:], bank[7][:, 0:2 * nw], wx_shift[:, 0:2 * nw], ALU.subtract).then_inc(s.fz_sb, 1)
                stt(out=f_n1[:], in0=bank[7][:, 2 * nw:NW], scalar=-2.0, in1=wx_shift[:, 2 * nw:NW],
                    op0=ALU.mult, op1=ALU.add).then_inc(s.fn1_sb, 1)
                dve.wait_ge(s.fz_sb, upto(f))
                tt(fz2[:], fz[:, 0:nw].rearrange("p (n r) -> p n r", r=NR),
                   fz[:, 0:nw].rearrange("p (n r) -> p n r", r=NR), ALU.mult).then_inc(s.fz2_sb, 1)
                dve.wait_ge(s.fn1_sb, upto(f))
                dve.wait_ge(s.x2_sb, upto(f))
                ts(f_n2[:], f_n1[:], x2sq[f.parity()][:], None, ALU.add).then_inc(s.fn2_sb, 1)
                dve.wait_ge(s.fz2_sb, upto(f))
                red(f_sc[:], fz2[:], AX_X, ALU.add)
                dve.wait_ge(s.fn2_sb, upto(f))
                nc.vector.reciprocal(f_n3[:], f_n2[:]).then_inc(s.fn3_sb, 1)
                dve.wait_ge(s.fn3_sb, upto(f))
                tt(f_s[:], f_sc[:], f_n3[:], ALU.mult).then_inc(s.fs_sb, 1)
                dve.wait_ge(s.fs_sb, upto(f))
                tt(f_u[:], f_s[:], xrow_sb[:, 0, :], ALU.subtract).then_inc(s.fu_sb, 1)
                dve.wait_ge(s.fu_sb, upto(f))
                tt(f_v[:], f_u[:], xrow_sb[:, 1, :], ALU.mult).then_inc(s.fv_sb, 1)

            def x_gate(f):
                dve.wait_ge(s.fe_sb, upto(f))
                ts(f_e1[:], f_e[:], 1.0, None, ALU.add).then_inc(s.fe1_sb, 1)
                dve.wait_ge(s.fe1_sb, upto(f))
                nc.vector.reciprocal(gate[:], f_e1[:]).then_inc(s.gate_sb, 1)
                dve.wait_ge(s.gate_sb, upto(f))
                red(g_max[:], gate[:], AX_X, ALU.max).then_inc(s.gmax_sb, 1)
                dve.wait_ge(s.gmax_sb, upto(f))
                stt(out=g_key[:], in0=gate[:], scalar=g_max[:], in1=xrow_sb[:, 2, :], op0=ALU.is_equal,
                    op1=ALU.mult).then_inc(s.gkey_sb, 1)
                ts(g_rest[:], g_max[:], -1.0, 2.0, ALU.mult, ALU.add)
                dve.wait_ge(s.gkey_sb, upto(f))
                red(g_kmax[:], g_key[:], AX_X, ALU.max).then_inc(s.gkmax_sb, 1)
                dve.wait_ge(s.gkmax_sb, upto(f))
                dve.wait_ge(s.LT_ps, upto(f, 1))
                ts(L[:, NX * NR:NL], g_key[:], g_kmax[:], g_max[:], ALU.is_equal, ALU.mult).then_inc(s.oh_sb, 1)
                dve.wait_ge(s.oh_sb, upto(f))
                tt(L[:, 0:NX * NR].rearrange("p (n r) -> p n r", r=NR),
                   fz[:, NX * NR:2 * NX * NR].rearrange("p (n r) -> p n r", r=NR),
                   L[:, NX * NR:NL].unsqueeze(2).broadcast_to([P, NX, NR]), ALU.mult).then_inc(s.L_sb, 1)

            def x_LT(f):
                dve.wait_ge(s.LT_ps, upto(f))
                dve.wait_ge(s.Y_ps, upto(f, 1))
                nc.vector.tensor_copy(LT[:], bank[5][0:NL, 0:P]).then_inc(s.LT_sb, 1)

            def x_y3(f):
                dve.wait_ge(s.Y_ps, upto(f))
                dve.wait_ge(s.x2_sb, upto(f))
                stt(out=y3[:], in0=x2[f.parity()][:], scalar=g_rest[:], in1=bank[6][:], op0=ALU.mult,
                    op1=ALU.add).then_inc(s.y3_sb, 1)
                dve.wait_ge(s.y3_sb, upto(f))
                norm_stats(f, y3, st3, mv3, ve3, s.st3_sb, s.mv3_sb, s.ve3_sb)

            def x_yo(f):
                dve.wait_ge(s.rs3_sb, upto(f))
                dve.wait_ge(s.y_out, stored(f))
                ts(yo[:], y3[:], mv3[:, 0:1], rs3[:], ALU.subtract, ALU.mult).then_inc(s.yo_sb, 1)

            nc.vector.memset(bias3[:], 0.0)
            nc.vector.memset(Mp[:], 0.0).then_inc(s.pads_set, 1)
            nc.vector.memset(zeros[:], 0.0).then_inc(s.pads_set, 1)
            nc.vector.memset(ones_f[:], 1.0).then_inc(s.pads_set, 1)
            nc.vector.memset(ones_bf[:], 1.0).then_inc(s.pads_set, 1)
            dve.wait_ge(s.const_in, CONST_IN)
            dve.wait_ge(s.pads_set, PADS)
            for n in range(3):
                cols = slice(n * E, (n + 1) * E)
                nc.vector.tensor_copy(bias3[0:1, cols], bias_in[n]).then_inc(s.bias_step, 1)
                dve.wait_ge(s.bias_step, 5 * n + 1)
                tt(bias_rest[n], bias_in[n], bias3[0:1, cols], ALU.subtract).then_inc(s.bias_step, 1)
                dve.wait_ge(s.bias_step, 5 * n + 2)
                nc.vector.tensor_copy(bias_mid[:, cols], bias_rest[n]).then_inc(s.bias_step, 1)
                nc.vector.tensor_copy(bias3[32:33, cols], bias_rest[n]).then_inc(s.bias_step, 1)
                dve.wait_ge(s.bias_step, 5 * n + 3)
                tt(bias3[64:65, cols], bias_rest[n], bias_mid[:, cols], ALU.subtract).then_inc(s.bias_step, 1)
            nw = NX * NR
            for c in range(CH):
                center = wx_sb[:, c, 2 * nw:NW]
                tt(wx_prod[:, c, 0:nw].rearrange("p (n r) -> p n r", r=NR),
                   wx_sb[:, c, 0:nw].rearrange("p (n r) -> p n r", r=NR),
                   center.unsqueeze(2).broadcast_to([P, NX, NR]), ALU.mult)
                last = tt(wx_prod[:, c, nw:2 * nw].rearrange("p (n r) -> p n r", r=NR),
                          wx_sb[:, c, nw:2 * nw].rearrange("p (n r) -> p n r", r=NR),
                          debias_sb[:, c, :].unsqueeze(2).broadcast_to([P, NX, NR]), ALU.mult)
            last.then_inc(s.prod_set, 1)
            tt(wx_prod[:, :, 2 * nw:NW], wx_sb[:, :, 2 * nw:NW], wx_sb[:, :, 2 * nw:NW],
               ALU.mult).then_inc(s.prod_set, 2)
            dve.wait_ge(s.shift_ps, 1)
            nc.vector.tensor_copy(wx_shift[:], bank[0][:, 0:NW]).then_inc(s.shift_set, 1)
            dve.wait_ge(s.shift_set, 1)
            for n in range(3):
                dve.wait_ge(s.high_set, n + 1)
                for c in range(CH):
                    last = tt(w_low[n][:, c, :], w_in[n][c], w_high[n][:, c, :], ALU.subtract)
                last.then_inc(s.low_set, 1)

            def step(a):
                b, c, e, f = a.older(1), a.older(2), a.older(3), a.older(4)
                if b.real():
                    for j in range(4):
                        a_max(b, j)
                if a.real():
                    p_low(a)
                if b.real():
                    for j in range(4):
                        a_rec(b, j)
                if e.real():
                    r_h(e)
                if c.real():
                    m_gs(c)
                if a.real():
                    p_q(a)
                if c.real():
                    m_logf(c)
                    m_scan(c, e)
                    m_parts(c, a)
                else:
                    if e.real():
                        r_var(e)
                    if a.real():
                        for part in range(3):
                            p_k(a, part)
                if f.real():
                    x_choose(f)
                if a.real():
                    p_VT(a)
                if f.real():
                    x_gate(f)
                if c.real():
                    m_acol(c)
                if a.real():
                    p_T(a, 0)
                if b.real():
                    a_low(b)
                if f.real():
                    x_LT(f)
                if a.real():
                    p_T(a, 1)
                if c.real():
                    m_C(c, 0)
                if f.real():
                    x_y3(f)
                if c.real():
                    m_C(c, 1)
                if e.real():
                    r_r2(e)
                if e.real():
                    r_x2(e)
                if f.real():
                    x_yo(f)
                if c.real():
                    m_C(c, 2)
                    m_C(c, 3)
                if b.real():
                    a_r1(b)
                    a_x1(b)

            steps(dve, step)


def kernel(**inputs):
    import ml_dtypes
    import numpy as np
    import concourse.bacc as bacc
    from concourse.bass_utils import run_bass_kernel_spmd as run

    i = {n: np.ascontiguousarray(a) for n, a in inputs.items()}

    pair = np.arange(E).reshape(H, D // 2, 2).transpose(0, 2, 1).reshape(E)
    token = np.arange(P) % 32 * 4 + np.arange(P) // 32
    inv = (1.0 / 10000.0 ** (np.arange(0, D, 2, dtype=np.float32) / np.float32(D))).astype(np.float32)
    freq = (token.astype(np.float32)[:, None] * inv).astype(np.float32).astype(np.float64)
    cos, sin = np.cos(freq), np.sin(freq)
    cos2, sin2 = np.concatenate([cos, cos], 1), np.concatenate([-sin, sin], 1)
    scale = D ** -0.5
    rope = np.stack([cos2 * scale, sin2 * scale, cos2, sin2], 1).astype(np.float32)
    row_i, col_i = np.arange(P) % 8, np.arange(4 * P) % 8
    mask_l, mask_r = np.zeros((P, P)), np.zeros((P, 4 * P))
    for n in range(8):
        mask_l[n] = row_i == n
        mask_r[n] = np.where(col_i == n, 0.0, -1e30)
    head_rows = np.zeros((80, H, P))
    for h in range(H):
        head_rows[[h, 32 + h, 64 + h], h] = 1.0
    bf16 = ml_dtypes.bfloat16

    def flat(a):
        return a.transpose(1, 0, 2).reshape(E, NX * NR)

    def gate_rows(a_i, a_f):
        rows = np.zeros((GW, a_i.shape[1]), a_i.dtype)
        rows[0:H], rows[32:GW] = a_i, a_f
        return rows

    arrays = {
        "x": i["x"], "ctx": i["ctx_2048"],
        "wq": i["L0_attn_Wq"][pair].T, "wk": i["L0_attn_Wk"][pair].T,
        "wv": i["L0_attn_Wv"].T, "wo": i["L0_attn_Wo"].T,
        "bqkv": np.concatenate([i["L0_attn_bq"][pair], i["L0_attn_bk"][pair], i["L0_attn_bv"]])[None],
        "bo": i["L0_attn_bo"][None],
        "rope": rope, "ident": np.eye(P, dtype=np.float32),
        "mask_l": mask_l.astype(bf16), "mask_r": mask_r.astype(bf16), "head_rows": head_rows.astype(bf16),
        "w_gate": gate_rows(i["L0_xattn_Wi"].T, i["L0_xattn_Wf"].T).T,
        "b_gate": gate_rows(i["L0_xattn_bi"][:, None], i["L0_xattn_bf"][:, None]),
        "ln_scale": i["L0_xattn_ln_scale"][None],
        "w_expert": np.concatenate([flat(i["L0_ffn_select_weight"]), flat(i["L0_ffn_lora_update"]),
                                    i["L0_ffn_select_mean_diff"].T], 1),
        "debias": i["L0_ffn_debias_w"].T,
        "degen": np.concatenate([i["L0_ffn_lora_degen"].transpose(0, 2, 1).reshape(NX * NR, E),
                                 i["L0_ffn_bias_w"]]),
        "expert_rows": np.stack([i["L0_ffn_imp_center"], i["L0_ffn_imp_slope"],
                                 np.arange(NX, 0, -1, dtype=np.float32)]),
    }
    nc = bacc.Bacc("TRN2", target_bir_lowering=False, num_devices=1)
    args, ins = {}, {}
    for name, a in arrays.items():
        a = np.ascontiguousarray(a)
        ins[f"in_{name}"] = a
        args[name] = nc.dram_tensor(f"in_{name}", a.shape, mybir.dt.from_np(a.dtype), kind="ExternalInput").ap()
    out = nc.dram_tensor("out_dram", (NT, P, E), F32, kind="ExternalOutput").ap()
    bass_decoder(nc, out=out, **args)
    return run(nc, [ins], core_ids=[0]).results[0]["out_dram"]
```
